# Optimizing a Trainium2 kernel written in Bass

```python
import numpy as np
import jax
import jax.numpy as jnp

def _softmax(x, axis=-1):
    return jax.nn.softmax(x, axis=axis)

def _gelu(x):
    return jax.nn.gelu(x, approximate=True)

def _silu(x):
    return jax.nn.silu(x)

def _sigmoid(x):
    return jax.nn.sigmoid(x)

def _layernorm(x, axis=-1, eps=1e-05):
    m = jnp.mean(x, axis=axis, keepdims=True)
    v = jnp.var(x, axis=axis, keepdims=True)
    return (x - m) / jnp.sqrt(v + eps)

def _scatter_add(tgt, idx, src, axis=0):
    return tgt.at[idx].add(src)

def _segment_sum(src, seg, n):
    return jax.ops.segment_sum(src, seg, n)
kernel_name = 'mk_adj_resnorm_d4_adj_r2_8d3b88'

def setup_inputs(seed: int=0):
    np.random.seed(seed)
    _w = jnp.asarray

    def _rec_inputs():
        import jax
        import jax.numpy as jnp
        _gk = jax.random.key(seed)
        x = 7.22e-05 + 1 * jax.random.normal(jax.random.fold_in(_gk, 1), (32, 256, 512), jnp.float32)
        _a = jax.random.bernoulli(jax.random.fold_in(_gk, 2), 0.015625, (256, 256))
        _a = jnp.logical_or(_a, jnp.swapaxes(_a, -1, -2))
        _a = jnp.logical_or(_a, jnp.eye(256, dtype=bool))
        _af = _a.astype(jnp.float32)
        adj = _af
        return (x, adj)
    x, adj = _rec_inputs()

    def _L0_gnn_setup():
        import jax, jax.numpy as jnp
        import numpy as np
        EPS = 1e-08

        def _row_stochastic_causal(A, causal_mask):
            A = A * causal_mask
            deg = jnp.maximum(A.sum(axis=-1, keepdims=True), EPS)
            return A / deg
        key = jax.random.key(seed)
        k = jax.random.split(key, 5)
        B, N, D = (4, 1024, 512)
        s = 1.0 / np.sqrt(D)
        h = jax.random.normal(k[0], (B, N, D), dtype=jnp.float32)
        W_lang = jax.random.normal(k[1], (D, D), dtype=jnp.float32) * s
        W_grav = jax.random.normal(k[2], (D, D), dtype=jnp.float32) * s
        W_V = jax.random.normal(k[3], (D, D), dtype=jnp.float32) * s
        W_O = jax.random.normal(k[4], (D, D), dtype=jnp.float32) * s
        causal_mask = jnp.tril(jnp.ones((N, N), dtype=jnp.float32))
        gate_logit = jnp.zeros((), jnp.float32)
        log_sigma = jnp.zeros((), jnp.float32)
        return {'h': h, 'causal_mask': causal_mask, 'W_lang': W_lang, 'W_grav': W_grav, 'W_V': W_V, 'W_O': W_O, 'gate_logit': gate_logit, 'log_sigma': log_sigma}
    _L0_gnn_all = _L0_gnn_setup()
    _L0_gnn_in = {k: v for k, v in _L0_gnn_all.items() if k in ('W_lang', 'W_grav', 'W_V', 'W_O', 'gate_logit', 'log_sigma')}
    del _L0_gnn_all

    def _L1_gnn_setup():
        import jax, jax.numpy as jnp
        import numpy as np
        NEG_SLOPE = 0.01
        key = jax.random.key(seed)
        k1, k2, k3, k4, k5 = jax.random.split(key, 5)
        B, C, N, O = (32, 256, 512, 256)
        x = jax.random.normal(k1, (B, C, N), dtype=jnp.float32)
        wq = jax.random.normal(k2, (C,), dtype=jnp.float32) * (1.0 / np.sqrt(C))
        wk = jax.random.normal(k3, (C,), dtype=jnp.float32) * (1.0 / np.sqrt(C))
        wm = jax.random.normal(k4, (O, C), dtype=jnp.float32) * (1.0 / np.sqrt(C))
        bm = jax.random.normal(k5, (O,), dtype=jnp.float32) * 0.01
        return {'x': x, 'wq': wq, 'wk': wk, 'wm': wm, 'bm': bm}
    _L1_gnn_all = _L1_gnn_setup()
    _L1_gnn_in = {k: v for k, v in _L1_gnn_all.items() if k in ('wq', 'wk', 'bm')}
    del _L1_gnn_all

    def _L2_gnn_setup():
        import jax, jax.numpy as jnp
        import numpy as np
        NEG_SLOPE = 0.01
        key = jax.random.key(seed)
        k1, k2, k3, k4, k5 = jax.random.split(key, 5)
        B, C, N, O = (32, 256, 512, 256)
        x = jax.random.normal(k1, (B, C, N), dtype=jnp.float32)
        wq = jax.random.normal(k2, (C,), dtype=jnp.float32) * (1.0 / np.sqrt(C))
        wk = jax.random.normal(k3, (C,), dtype=jnp.float32) * (1.0 / np.sqrt(C))
        wm = jax.random.normal(k4, (O, C), dtype=jnp.float32) * (1.0 / np.sqrt(C))
        bm = jax.random.normal(k5, (O,), dtype=jnp.float32) * 0.01
        return {'x': x, 'wq': wq, 'wk': wk, 'wm': wm, 'bm': bm}
    _L2_gnn_all = _L2_gnn_setup()
    _L2_gnn_in = {k: v for k, v in _L2_gnn_all.items() if k in ('wq', 'wk', 'bm')}
    del _L2_gnn_all

    def _L3_gnn_setup():
        import jax, jax.numpy as jnp
        import numpy as np
        DIM = 199
        K_HOP = 3

        def _khop_support(n, k):
            A = np.eye(n, dtype=np.float64)
            idx = np.arange(n)
            A[idx, (idx + 1) % n] = 1.0
            A[(idx + 1) % n, idx] = 1.0
            S = np.linalg.matrix_power(A, k)
            return (S > 0).astype(np.float32)
        key = jax.random.key(seed)
        kx, kk = jax.random.split(key)
        batch, n, f = (128, DIM, 512)
        x = jax.random.normal(kx, (batch, n, f), dtype=jnp.float32)
        support = jnp.asarray(_khop_support(n, K_HOP))
        limit = float(np.sqrt(6.0 / (n + n)))
        kernel = jax.random.uniform(kk, (n, n), minval=-limit, maxval=limit, dtype=jnp.float32)
        bias = jnp.zeros((f,), dtype=jnp.float32)
        return {'x': x, 'support': support, 'kernel': kernel, 'bias': bias}
    _L3_gnn_all = _L3_gnn_setup()
    _L3_gnn_in = {k: v for k, v in _L3_gnn_all.items() if k in ('bias',)}
    del _L3_gnn_all
    return {'x': x, 'adj': adj, 'L0_gnn_W_lang': _L0_gnn_in['W_lang'], 'L0_gnn_W_grav': _L0_gnn_in['W_grav'], 'L0_gnn_W_V': _L0_gnn_in['W_V'], 'L0_gnn_W_O': _L0_gnn_in['W_O'], 'L0_gnn_gate_logit': _L0_gnn_in['gate_logit'], 'L0_gnn_log_sigma': _L0_gnn_in['log_sigma'], 'L1_gnn_wq': _L1_gnn_in['wq'], 'L1_gnn_wk': _L1_gnn_in['wk'], 'L1_gnn_bm': _L1_gnn_in['bm'], 'L2_gnn_wq': _L2_gnn_in['wq'], 'L2_gnn_wk': _L2_gnn_in['wk'], 'L2_gnn_bm': _L2_gnn_in['bm'], 'L3_gnn_bias': _L3_gnn_in['bias']}

def reference(x, adj, L0_gnn_W_lang, L0_gnn_W_grav, L0_gnn_W_V, L0_gnn_W_O, L0_gnn_gate_logit, L0_gnn_log_sigma, L1_gnn_wq, L1_gnn_wk, L1_gnn_bm, L2_gnn_wq, L2_gnn_wk, L2_gnn_bm, L3_gnn_bias):
    import jax
    import jax.numpy as jnp

    def _L0_gnn_ref(h, causal_mask, W_lang, W_grav, W_V, W_O, gate_logit, log_sigma):
        import jax, jax.numpy as jnp
        import numpy as np
        EPS = 1e-08

        def _row_stochastic_causal(A, causal_mask):
            A = A * causal_mask
            deg = jnp.maximum(A.sum(axis=-1, keepdims=True), EPS)
            return A / deg
        z_l = jnp.einsum('bnd,ed->bne', h, W_lang)
        z_g = jnp.einsum('bnd,ed->bne', h, W_grav)
        v = jnp.einsum('bnd,ed->bne', h, W_V)
        N = h.shape[-2]
        not_eye = 1.0 - jnp.eye(N, dtype=h.dtype)
        zn = z_l / jnp.maximum(jnp.linalg.norm(z_l, axis=-1, keepdims=True), EPS)
        A_l = jnp.maximum(jnp.einsum('bnd,bmd->bnm', zn, zn), 0.0) * not_eye
        sq = jnp.sum(z_g * z_g, axis=-1, keepdims=True)
        d2 = jnp.maximum(sq + jnp.swapaxes(sq, -1, -2) - 2.0 * jnp.einsum('bnd,bmd->bnm', z_g, z_g), 0.0)
        sigma = jnp.exp(log_sigma)
        A_g = jnp.exp(-d2 / (2.0 * sigma * sigma)) * not_eye
        K_l = _row_stochastic_causal(A_l, causal_mask)
        K_g = _row_stochastic_causal(A_g, causal_mask)
        w_l = jax.nn.sigmoid(gate_logit)
        K = w_l * K_l + (1.0 - w_l) * K_g
        out = jnp.einsum('bnm,bmd->bnd', K, v)
        return jnp.einsum('bnd,ed->bne', out, W_O)

    def _L1_gnn_ref(x, wq, wk, wm, bm):
        import jax, jax.numpy as jnp
        import numpy as np
        NEG_SLOPE = 0.01
        q = jnp.einsum('c,bcn->bn', wq, x)
        k = jnp.einsum('c,bcn->bn', wk, x)
        scores = q[:, None, :] + k[:, :, None]
        scores = jnp.where(scores > 0, scores, NEG_SLOPE * scores)
        att = jax.nn.softmax(scores, axis=-1)
        agg = jnp.einsum('bcn,bmn->bcm', x, att)
        out = jnp.einsum('oc,bcm->bom', wm, agg) + bm[None, :, None]
        return jax.nn.relu(out)

    def _L2_gnn_ref(x, wq, wk, wm, bm):
        import jax, jax.numpy as jnp
        import numpy as np
        NEG_SLOPE = 0.01
        q = jnp.einsum('c,bcn->bn', wq, x)
        k = jnp.einsum('c,bcn->bn', wk, x)
        scores = q[:, None, :] + k[:, :, None]
        scores = jnp.where(scores > 0, scores, NEG_SLOPE * scores)
        att = jax.nn.softmax(scores, axis=-1)
        agg = jnp.einsum('bcn,bmn->bcm', x, att)
        out = jnp.einsum('oc,bcm->bom', wm, agg) + bm[None, :, None]
        return jax.nn.relu(out)

    def _L3_gnn_ref(x, support, kernel, bias):
        import jax, jax.numpy as jnp
        import numpy as np
        DIM = 199
        K_HOP = 3

        def _khop_support(n, k):
            A = np.eye(n, dtype=np.float64)
            idx = np.arange(n)
            A[idx, (idx + 1) % n] = 1.0
            A[(idx + 1) % n, idx] = 1.0
            S = np.linalg.matrix_power(A, k)
            return (S > 0).astype(np.float32)
        W = support * kernel
        out = jnp.einsum('bnf,nm->bmf', x, W)
        out = out + bias
        return out
    x = _layernorm(x + _L0_gnn_ref(x, adj, L0_gnn_W_lang, L0_gnn_W_grav, L0_gnn_W_V, L0_gnn_W_O, L0_gnn_gate_logit, L0_gnn_log_sigma), axis=-1)
    x = _layernorm(x + _L1_gnn_ref(x, L1_gnn_wq, L1_gnn_wk, adj, L1_gnn_bm), axis=-1)
    x = _layernorm(x + _L2_gnn_ref(x, L2_gnn_wq, L2_gnn_wk, adj, L2_gnn_bm), axis=-1)
    x = _layernorm(x + _L3_gnn_ref(x, adj, adj, L3_gnn_bias), axis=-1)
    return x

_drawn_inputs = setup_inputs


def setup_inputs(seed=0):
    import zlib

    import numpy as np

    out = dict(_drawn_inputs(seed))
    spreads = {'L3_gnn_bias': (0.0, 0.281)}
    factors = {'L1_gnn_bm': 46.448, 'L2_gnn_bm': 48.266}
    for name, (base, spread) in spreads.items():
        noise = np.random.default_rng([zlib.crc32(name.encode()), seed]).standard_normal(out[name].shape)
        drawn = base * np.exp(spread * noise) if base else spread * noise
        out[name] = jnp.asarray(drawn.astype(out[name].dtype))
    for name, factor in factors.items():
        out[name] = (out[name] * factor).astype(out[name].dtype)
    return out
```

```python
from contextlib import ExitStack

import concourse.bass as bass
from concourse import mybir

F32 = mybir.dt.float32
F32R = mybir.dt.float32r
ALU = mybir.AluOpType
ACT = mybir.ActivationFunctionType
AX_X = mybir.AxisListType.X

P = 128
LEAK = 0.01
LN_EPS = 1e-5
EPS = 1e-8

ORDER = [
    ("ZL", 0), ("Y", 0, 0), ("ZL", 1), ("QK", 0, 0), ("ZL", 2), ("ATT", 0, 0), ("Y", 0, 1), ("ZL", 3),
    ("QK", 0, 1), ("GL", 0), ("U", 0, 0), ("ATT", 0, 1), ("DEN", 0, 0), ("GL", 1), ("RD", 0, 0), ("RB", 0),
    ("V", 0), ("RES", 0, 0), ("RB", 1), ("U", 0, 1), ("NRM", 0, 0), ("DEN", 0, 1), ("V", 1), ("RD", 0, 1),
    ("Y", 1, 0), ("RES", 0, 1), ("V", 2), ("QK", 1, 0), ("NRM", 0, 1), ("V", 3), ("ATT", 1, 0), ("Y", 1, 1),
    ("ZG", 0), ("QK", 1, 1), ("ZG", 1), ("U", 1, 0), ("ATT", 1, 1), ("DEN", 1, 0), ("ZG", 2), ("RD", 1, 0),
    ("ZG", 3), ("RES", 1, 0), ("XT", 0), ("GG", 0), ("U", 1, 1), ("NRM", 1, 0), ("DEN", 1, 1), ("HB", 0),
    ("GG", 1), ("RD", 1, 1), ("RES", 1, 1), ("EG", 0), ("HB", 1), ("L3", 0), ("NRM", 1, 1), ("XT", 1),
    ("EG", 1), ("KT", 0), ("L3N", 0), ("L3", 1), ("KT", 1), ("KV", 0), ("L3N", 1), ("KV", 1), ("KVN", 0),
    ("KVN", 1),
]
FRONT = {"XT", "ZL", "ZG", "V", "GL", "GG", "RB", "HB", "EG", "KT", "KV", "KVN"}


class Signal:

    def __init__(self, sem, stages, each=1, step=1):
        self.sem, self.each, self.step = sem, each, step
        self.at = {key: n for n, key in enumerate(k for k in ORDER if k[0] in stages)}
        self.per_pair = len(self.at) * each

    def after(self, pair, key, k=None):
        k = self.each if k is None else k
        return (pair * self.per_pair + self.at[key] * self.each + k) * self.step


class Bank:

    def __init__(self, tensor, full, free, uses):
        self.t, self.full, self.free = tensor, full, free
        self.at = {key: n for n, key in enumerate(uses)}
        self.n = len(uses)

    def filled(self, pair, key):
        return pair * self.n + self.at[key] + 1

    read = filled

    def before(self, pair, key):
        return pair * self.n + self.at[key]


class Chain:

    def __init__(self, sem):
        self.sem, self.k, self.n, self.pair = sem, 0, None, 0

    def begin(self, pair):
        if self.n is None and not (isinstance(pair, int) and pair == 0):
            self.n = self.k
        self.pair, self.k = pair, 0

    def link(self, eng, ins):
        ins.then_inc(self.sem, 1)
        self.k += 1
        base = 0 if self.n is None else self.pair * self.n
        eng.wait_ge(self.sem, base + self.k)


def uses_of(bank):
    kind, n = bank
    out = []
    for key in ORDER:
        s, a = key[0], key[1:]
        if kind == "P":
            if s in ("ZL", "ZG", "V") and a[0] % 2 == n:
                out.append(key)
            if s in ("RB", "HB", "KT") and a[0] == n:
                out.append(key)
            if s == "KV" and a[0] == 1:
                out.append(key)
        if kind == "G":
            if s in ("GL", "GG") and a[0] == n:
                out.append(key)
            if s == "KV" and a[0] == 0:
                out.append(key)
        if kind == "Y":
            if s == "Y":
                out += [key + (n,), key + (n + 2,)]
            if s == "QK" or (s == "DEN" and n == 0) or (s == "RD" and n == 1):
                out.append(key)
        if kind == "U" and s in ("U", "L3"):
            out.append(key)
    return out


def resnorm_kernel(nc, xn, xt, adj, adjq, w_l, w_g, w_v, w_o, gate, sigma, bm1, bm2, bias3, ident_in, out):
    PAIRS = xn.shape[0]
    D = xn.shape[3]
    KD = D // P
    N = adj.shape[0]
    NT = N // P
    AQ = adjq.shape[1]
    YW = N + 2

    with ExitStack() as ctx:
        def sb(name, shape, dt=F32):
            return ctx.enter_context(nc.sbuf_tensor(name, shape, dt))

        def sem(name):
            return ctx.enter_context(nc.semaphore(name))

        wl_h, wl_l = sb("wl_h", [P, KD, D], F32R), sb("wl_l", [P, KD, D], F32R)
        wg_h, wg_l = sb("wg_h", [P, KD, D], F32R), sb("wg_l", [P, KD, D], F32R)
        wv_h, wv_l = sb("wv_h", [P, KD, D], F32R), sb("wv_l", [P, KD, D], F32R)
        aq_h, aq_l = sb("aq_h", [P, NT, AQ], F32R), sb("aq_l", [P, NT, AQ], F32R)
        a2_h, a2_l = sb("a2_h", [P, NT, N], F32R), sb("a2_l", [P, NT, N], F32R)
        offdiag = sb("offdiag", [P, NT, N])
        ident = sb("ident", [P, P])
        ones = sb("ones", [P, 1])
        bias_bc = sb("bias_bc", [P, D])
        bm = sb("bm", [P, 2, NT])
        w_lang_col, w_grav_col = sb("w_lang_col", [P, 1]), sb("w_grav_col", [P, 1])
        inv_s2 = sb("inv_s2", [P, 1])
        eps_col = sb("eps_col", [P, 1])
        tiny = sb("tiny", [P, 4])
        carrier = sb("carrier", [P, 2])

        xt_in = sb("xt_in", [P, 2, D])
        xt_h, xt_l = sb("xt_h", [P, KD, D], F32R), sb("xt_l", [P, KD, D], F32R)
        z_h, z_l = sb("z_h", [P, KD, D], F32R), sb("z_l", [P, KD, D], F32R)
        v_h, v_l = sb("v_h", [P, KD, D], F32R), sb("v_l", [P, KD, D], F32R)
        lang = sb("lang", [P, 2, NT, N])
        grav = sb("grav", [P, 2, NT, N])
        half_sq_bc = sb("half_sq_bc", [P, 2, N])
        kt_h, kt_l = sb("kt_h", [P, 2, NT, N], F32R), sb("kt_l", [P, 2, NT, N], F32R)
        cols = sb("cols", [P, 2, 12, NT])
        SS, LNS, R, SQ, HSQ, DEGL, CL, DEGG, CG = range(9)

        x1 = sb("x1", [P, 2 * NT, D])
        x2 = sb("x2", [P, 2 * NT, D])
        x_h, x_l = sb("x_h", [P, 2 * NT, D], F32R), sb("x_l", [P, 2 * NT, D], F32R)
        stats = sb("stats", [P, 2, 2, NT, 6])
        mean_var = sb("mean_var", [P, 2, 2, NT, 2])
        log_var = sb("log_var", [P, 2, 2, NT])
        rstd = sb("rstd", [P, 2, 2, NT])

        y_h, y_l = sb("y_h", [P, 2, KD, YW], F32R), sb("y_l", [P, 2, KD, YW], F32R)
        qk = sb("qk", [P, 2, KD, 2])
        qs = sb("qs", [P, 2, 2 + KD])
        ab = sb("ab", [P, 2, 2, KD])
        s_neg, s_pos = sb("s_neg", [P, D]), sb("s_pos", [P, D])
        att = sb("att", [P, KD, D])
        att_h, att_l = sb("att_h", [P, KD, D], F32R), sb("att_l", [P, KD, D], F32R)
        den_sum = sb("den_sum", [P, D])
        inv_den = sb("inv_den", [P, KD])
        inv_den_bc = sb("inv_den_bc", [P, D])
        u = sb("u", [P, NT, D])

        def bank(kind, n):
            name = f"{kind}{n}".lower()
            t = ctx.enter_context(nc.psum_tensor("bank_" + name, [P, D], F32))
            return Bank(t, sem(name + "_full"), sem(name + "_free"), uses_of((kind, n)))

        pb = [bank("P", 0), bank("P", 1)]
        gb = [bank("G", 0), bank("G", 1)]
        yb = [bank("Y", 0), bank("Y", 1)]
        ub = [bank("U", 0), bank("U", 1)]

        w_in, setup_wov, setup_act, setup_dve = sem("w_in"), sem("setup_wov"), sem("setup_act"), sem("setup_dve")
        w_in2 = sem("w_in2")
        small_in, setup_own = sem("small_in"), sem("setup_own")
        xt_loaded = Signal(sem("xt_loaded"), ("XT",), step=16)
        x0_loaded = [sem("x0_loaded_0"), sem("x0_loaded_1")]
        stored = [sem("stored_0"), sem("stored_1")]
        xt_hi = Signal(sem("xt_hi"), ("XT",))
        xt_lo = Signal(sem("xt_lo"), ("XT",))
        proj_hi = Signal(sem("proj_hi"), ("ZL", "ZG", "V"))
        lang_sq = Signal(sem("lang_sq"), ("GL",))
        lang_r = Signal(sem("lang_r"), ("GL",))
        grav_hsq = Signal(sem("grav_hsq"), ("GG",))
        grav_d = Signal(sem("grav_d"), ("HB",))
        grav_e = Signal(sem("grav_e"), ("HB",))
        graph = Signal(sem("graph"), ("EG",))
        kt_hi = Signal(sem("kt_hi"), ("KT",))
        added = Signal(sem("added"), ("RES",), 2)
        var_known = [Signal(sem("f_var"), ("KV",)), Signal(sem("b_var"), ("RES", "L3"))]
        rstd_known = [Signal(sem("f_rstd"), ("KV",)), Signal(sem("b_rstd"), ("RES", "L3"))]
        normed = [Signal(sem("f_normed"), ("KVN",), 2), Signal(sem("b_normed"), ("NRM", "L3N"), 2)]
        x_hi = [Signal(sem("f_x_hi"), ("KVN",)), Signal(sem("b_x_hi"), ("NRM",))]
        x_lo = [Signal(sem("f_x_lo"), ("KVN",), 2), Signal(sem("b_x_lo"), ("NRM",), 2)]
        biased = Signal(sem("biased"), ("L3",), 2)
        y_hi = Signal(sem("y_hi"), ("Y",), 4)
        qk_cols = Signal(sem("qk_cols"), ("Y",))
        q_max = Signal(sem("q_max"), ("QK",))
        factors = Signal(sem("factors"), ("QK",))
        att_low = Signal(sem("att_low"), ("ATT",), 4)
        att_val = Signal(sem("att_val"), ("ATT",), 4)
        att_hi = Signal(sem("att_hi"), ("ATT",), 4)
        att_lo = Signal(sem("att_lo"), ("ATT",), 4)
        summed = Signal(sem("summed"), ("ATT",))
        relued = Signal(sem("relued"), ("RES",), 2)
        dve_f, dve_b = Chain(sem("dve_f")), Chain(sem("dve_b"))
        act_f, act_b = Chain(sem("act_f")), Chain(sem("act_b"))
        pool_b = Chain(sem("pool_b"))

        def f32(ap):
            return ap.bitcast(F32)

        def y_cols(layer, ot):
            at = (2 if layer == 0 else 0) + ot * P
            return slice(at, at + P)

        def q_cols(layer):
            return slice(0, 2) if layer == 0 else slice(N, N + 2)

        def schedule(eng, stages, chains):
            fchains, bchains = chains

            def one(front, back, ahead=True):
                for c in fchains:
                    if front is not None:
                        c.begin(front)
                for c in bchains:
                    if back is not None:
                        c.begin(back)
                for key in ORDER:
                    do = stages.get(key[0])
                    if do is None:
                        continue
                    if key[0] == "XT":
                        if front is not None and ahead:
                            do(front + 1, *key[1:])
                    elif key[0] in FRONT:
                        if front is not None:
                            do(front, *key[1:])
                    elif back is not None:
                        do(back, *key[1:])

            if "XT" in stages:
                stages["XT"](0, 0)
                stages["XT"](0, 1)
            one(0, None)
            one(1, 0)
            with eng.Fori(2, PAIRS - 1) as i:
                one(i, i - 1)
            one(PAIRS - 1, PAIRS - 2, ahead=False)
            one(None, PAIRS - 1)

        def first(pair):
            return isinstance(pair, int) and pair == 0

        def dve_carrier():
            nc.vector.memset(carrier[:, 0:1], 0.0)

        def pool_carrier():
            nc.gpsimd.tensor_tensor(carrier[:, 1:2], ones[:, 0:1], ones[:, 0:1], ALU.mult)

        block = ctx.enter_context(nc.Block())

        @block.sync
        def _(sp):
            for n, (t, src) in enumerate(((ident, ident_in), (offdiag, adj.rearrange("(t p) m -> p t m", p=P)),
                                          (bias_bc, bias3), (bm[:, 0, :], bm1), (bm[:, 1, :], bm2),
                                          (tiny[:, 0:1], gate), (tiny[:, 1:2], sigma),
                                          (x_small_view(xt_in, NT, AQ), adjq.rearrange("(t p) m -> p t m", p=P)))):
                sp.dma_start(t if n in (3, 4, 5, 6, 7) else t[:], src).then_inc(small_in, 16)
            sp.dma_start(x1[:], w_o.rearrange("(t p) m -> p t m", p=P)).then_inc(w_in, 16)
            sp.dma_start(x2[:], w_v.rearrange("(t p) m -> p t m", p=P)).then_inc(w_in, 16)
            sp.dma_start(att[:], w_l.rearrange("(t p) m -> p t m", p=P)).then_inc(w_in2, 16)
            sp.wait_ge(setup_dve, 2)
            sp.dma_start(att[:], w_g.rearrange("(t p) m -> p t m", p=P)).then_inc(w_in2, 16)

            def load_xt(pair, c):
                if c == 1:
                    sp.wait_ge(xt_lo.sem, xt_lo.after(pair, ("XT", 0)))
                elif not first(pair):
                    sp.wait_ge(xt_lo.sem, xt_lo.after(pair - 1, ("XT", 1)))
                else:
                    sp.wait_ge(setup_dve, 5)
                sp.dma_start(xt_in[:], xt[pair, :, 2 * c:2 * c + 2, :]).then_inc(xt_loaded.sem, 16)

            def load_x0(pair, h):
                if first(pair):
                    sp.wait_ge(setup_wov, 4)
                else:
                    sp.wait_ge(added.sem, added.after(pair - 1, ("RES", 0, h)))
                sp.dma_start(x1[:, NT * h:NT * h + NT, :], xn[pair, :, NT * h:NT * h + NT, :]).then_inc(x0_loaded[h], 16)

            def store(pair, h):
                sp.wait_ge(normed[1].sem, normed[1].after(pair, ("L3N", h)))
                sp.dma_start(out[pair, :, NT * h:NT * h + NT, :], x2[:, NT * h:NT * h + NT, :]).then_inc(stored[h], 16)

            load_xt(0, 0)
            load_x0(0, 0)
            load_x0(0, 1)
            load_xt(0, 1)
            load_xt(1, 0)
            load_xt(1, 1)

            def one(front, back, ahead):
                for key in ORDER:
                    if key[0] == "RES" and key[1] == 0 and front is not None:
                        load_x0(front, key[2])
                    if key[0] == "XT" and ahead:
                        load_xt(front + 1, key[1])
                    if key[0] == "L3N":
                        store(back, key[1])

            one(1, 0, True)
            with sp.Fori(2, PAIRS - 1) as i:
                one(i, i - 1, True)
            one(PAIRS - 1, PAIRS - 2, False)
            one(None, PAIRS - 1, False)
            for h in range(2):
                sp.wait_ge(stored[h], 16 * PAIRS)

        @block.tensor
        def _(pe):
            def split_product(outap, pairs, start, stop):
                last = None
                n = 3 * len(pairs)
                m = 0
                for sh, sl, mh, ml in pairs:
                    for a, b in ((sh, mh), (sh, ml), (sl, mh)):
                        last = pe.matmul(outap, a, b, start=start and m == 0, stop=stop and m == n - 1)
                        m += 1
                return last

            def take(b, pair, key):
                if not (first(pair) and b.at[key] == 0):
                    pe.wait_ge(b.free, b.before(pair, key))

            pe.wait_ge(w_in, 32)
            for k in range(KD):
                for e in range(KD):
                    mm = pe.matmul([pb, gb][k // 2][k % 2].t[:], x2[:, e, k * P:(k + 1) * P], x1[:, e, :],
                                   start=e == 0, stop=e == KD - 1)
                mm.then_inc(setup_wov, 1)
            pe.wait_ge(setup_dve, 9)

            def project(kind, weights_h, weights_l):
                def do(pair, e):
                    key = (kind, e)
                    b = pb[e % 2]
                    take(b, pair, key)
                    if key == ("ZL", 0):
                        pe.wait_ge(xt_lo.sem, xt_lo.after(pair, ("XT", 1)))
                    c = slice(e * P, (e + 1) * P)
                    if kind == "V":
                        ops = [(xt_h[:, k, c], xt_l[:, k, c], weights_h[:, k, :], weights_l[:, k, :]) for k in range(KD)]
                    else:
                        ops = [(weights_h[:, k, c], weights_l[:, k, c], xt_h[:, k, :], xt_l[:, k, :]) for k in range(KD)]
                    split_product(b.t[:], ops, True, True).then_inc(b.full, 1)
                return do

            def gram(kind, z):
                def do(pair, h):
                    key = (kind, h)
                    b = gb[h]
                    take(b, pair, key)
                    for n in (2, 3):
                        pe.wait_ge(pb[n % 2].free, pb[n % 2].read(pair, (z, n)))
                    m = slice(h * N, (h + 1) * N)
                    for j in range(NT):
                        c = slice(h * N + j * P, h * N + (j + 1) * P)
                        mm = split_product(b.t[:, j * N:(j + 1) * N],
                                           [(z_h[:, k, c], z_l[:, k, c], z_h[:, k, m], z_l[:, k, m]) for k in range(KD)],
                                           True, True)
                    mm.then_inc(b.full, 1)
                return do

            def spread(outap, col):
                return pe.transpose(outap, col.broadcast_to([P, P]), ident[:])

            def rb(pair, h):
                take(pb[h], pair, ("RB", h))
                pe.wait_ge(lang_r.sem, lang_r.after(pair, ("GL", h)))
                for j in range(NT):
                    mm = spread(pb[h].t[:, j * P:(j + 1) * P], cols[:, h, R, j:j + 1])
                mm.then_inc(pb[h].full, 1)

            def hb(pair, h):
                take(pb[h], pair, ("HB", h))
                pe.wait_ge(grav_hsq.sem, grav_hsq.after(pair, ("GG", h)))
                for j in range(NT):
                    mm = spread(pb[h].t[:, j * P:(j + 1) * P], cols[:, h, HSQ, j:j + 1])
                mm.then_inc(pb[h].full, 1)

            def kt(pair, h):
                take(pb[h], pair, ("KT", h))
                pe.wait_ge(graph.sem, graph.after(pair, ("EG", h)))
                for mt in range(NT):
                    for j in range(NT):
                        mm = pe.transpose(pb[h].t[:, mt * N + j * P:mt * N + (j + 1) * P],
                                          lang[:, h, j, mt * P:(mt + 1) * P], ident[:])
                mm.then_inc(pb[h].full, 1)

            def kv(pair, h):
                pe.wait_ge(pb[h].free, pb[h].read(pair, ("KT", h)))
                for j in range(NT):
                    b = (gb, pb)[h][j]
                    take(b, pair, ("KV", h))
                    c = slice(j * P, (j + 1) * P)
                    split_product(b.t[:], [(kt_h[:, h, mt, c], kt_l[:, h, mt, c], v_h[:, NT * h + mt, :],
                                            v_l[:, NT * h + mt, :]) for mt in range(NT)],
                                  True, True).then_inc(b.full, 1)

            def y(pair, layer, h):
                if layer == 0:
                    pe.wait_ge(x_lo[0].sem, x_lo[0].after(pair, ("KVN", h)))
                else:
                    pe.wait_ge(x_lo[1].sem, x_lo[1].after(pair, ("NRM", 0, h)))
                m = slice(0, YW) if layer == 0 else slice(2, 2 + YW)
                for i in range(KD):
                    b = yb[i % 2]
                    take(b, pair, ("Y", layer, h, i))
                    c = slice(i * P, (i + 1) * P)
                    split_product(b.t[:, 0:YW], [(x_h[:, NT * h + t, c], x_l[:, NT * h + t, c], aq_h[:, t, m], aq_l[:, t, m])
                                                 for t in range(NT)], True, True).then_inc(b.full, 1)

            def qk_rows(pair, layer, h):
                key = ("QK", layer, h)
                pe.wait_ge(qk_cols.sem, qk_cols.after(pair, ("Y", layer, h)))
                for w in range(2):
                    take(yb[w], pair, key)
                    for i in range(KD):
                        mm = spread(yb[w].t[:, i * P:(i + 1) * P], qk[:, h, i, w:w + 1])
                    mm.then_inc(yb[w].full, 1)

            def apply(pair, layer, h):
                for i in range(KD):
                    pe.wait_ge(att_lo.sem, att_lo.after(pair, ("ATT", layer, h), i + 1))
                    for ot in range(NT):
                        if i == 0:
                            take(ub[ot], pair, ("U", layer, h))
                        c = y_cols(layer, ot)
                        mm = split_product(ub[ot].t[:], [(y_h[:, h, i, c], y_l[:, h, i, c], att_h[:, i, :], att_l[:, i, :])],
                                           i == 0, i == KD - 1)
                        if i == KD - 1:
                            mm.then_inc(ub[ot].full, 1)

            def den(pair, layer, h):
                take(yb[0], pair, ("DEN", layer, h))
                pe.wait_ge(summed.sem, summed.after(pair, ("ATT", layer, h)))
                for i in range(KD):
                    mm = pe.matmul(yb[0].t[:, i:i + 1], den_sum[:, i * P:(i + 1) * P], ones[:, 0:1], start=True, stop=True)
                mm.then_inc(yb[0].full, 1)

            def rd(pair, layer, h):
                take(yb[1], pair, ("RD", layer, h))
                pe.wait_ge(yb[0].free, yb[0].read(pair, ("DEN", layer, h)))
                for i in range(KD):
                    mm = spread(yb[1].t[:, i * P:(i + 1) * P], inv_den[:, i:i + 1])
                mm.then_inc(yb[1].full, 1)

            def l3(pair, h):
                pe.wait_ge(x_lo[1].sem, x_lo[1].after(pair, ("NRM", 1, h)))
                for mt in range(NT):
                    take(ub[mt], pair, ("L3", h))
                    c = slice(mt * P, (mt + 1) * P)
                    split_product(ub[mt].t[:], [(a2_h[:, t, c], a2_l[:, t, c], x_h[:, NT * h + t, :], x_l[:, NT * h + t, :])
                                                for t in range(NT)], True, True).then_inc(ub[mt].full, 1)

            schedule(pe, {"ZL": project("ZL", wl_h, wl_l), "ZG": project("ZG", wg_h, wg_l), "V": project("V", wv_h, wv_l),
                          "GL": gram("GL", "ZL"), "GG": gram("GG", "ZG"), "RB": rb, "HB": hb, "KT": kt, "KV": kv,
                          "Y": y, "QK": qk_rows, "U": apply, "DEN": den, "RD": rd, "L3": l3}, ((), ()))

        @block.scalar
        def _(act):
            act.wait_ge(small_in, 16 * 8)
            nc.scalar.activation(aq_h[:], x_small_view(xt_in, NT, AQ), ACT.Copy).then_inc(setup_act, 1)
            nc.scalar.activation(tiny[:, 2:3], tiny[:, 0:1], ACT.Exp, scale=-1.0).then_inc(setup_act, 1)
            nc.scalar.activation(inv_s2[:], tiny[:, 1:2], ACT.Exp, scale=-2.0).then_inc(setup_act, 1)
            act.wait_ge(w_in2, 16)
            nc.scalar.activation(wl_h[:], att[:], ACT.Copy).then_inc(setup_act, 1)
            for k in range(KD):
                act.wait_ge(setup_wov, k + 1)
                nc.scalar.activation(wv_h[:, k, :], [pb, gb][k // 2][k % 2].t[:], ACT.Copy).then_inc(setup_act, 1)
            act.wait_ge(w_in2, 32)
            nc.scalar.activation(wg_h[:], att[:], ACT.Copy).then_inc(setup_act, 1)
            act.wait_ge(setup_dve, 4)
            nc.scalar.activation(a2_h[:], grav[:, 0, :, :], ACT.Copy).then_inc(setup_act, 1)

            def xt_split(pair, c):
                act.wait_ge(xt_loaded.sem, xt_loaded.after(pair, ("XT", c)))
                if not first(pair):
                    last = max((("ZL", 3), ("ZG", 3), ("V", 3)), key=ORDER.index)
                    act.wait_ge(pb[1].full, pb[1].filled(pair - 1, last))
                nc.scalar.activation(xt_h[:, 2 * c:2 * c + 2, :], xt_in[:], ACT.Copy).then_inc(xt_hi.sem, 1)

            def project(kind, dst):
                def do(pair, e):
                    b = pb[e % 2]
                    act.wait_ge(b.full, b.filled(pair, (kind, e)))
                    if kind == "ZG":
                        act.wait_ge(gb[1].full, gb[1].filled(pair, ("GL", 1)))
                    elif kind == "ZL" and not first(pair):
                        act.wait_ge(gb[1].full, gb[1].filled(pair - 1, ("GG", 1)))
                    elif kind == "V" and not first(pair):
                        act.wait_ge(pb[1].full, pb[1].filled(pair - 1, ("KV", 1)))
                    nc.scalar.activation(dst[:, e, :], b.t[:], ACT.Copy).then_inc(proj_hi.sem, 1)
                return do

            def gl(pair, h):
                act.wait_ge(lang_sq.sem, lang_sq.after(pair, ("GL", h)))
                act_f.link(act, nc.scalar.activation(cols[:, h, LNS, :], cols[:, h, SS, :], ACT.Ln))
                nc.scalar.activation(cols[:, h, R, :], cols[:, h, LNS, :], ACT.Exp, scale=-0.5).then_inc(lang_r.sem, 1)

            def hb(pair, h):
                act.wait_ge(pb[h].full, pb[h].filled(pair, ("HB", h)))
                nc.scalar.activation(half_sq_bc[:, h, :], pb[h].t[:, 0:N], ACT.Copy).then_inc(pb[h].free, 1)
                act.wait_ge(grav_d.sem, grav_d.after(pair, ("HB", h)))
                nc.scalar.activation(grav[:, h, :, :], grav[:, h, :, :], ACT.Exp, scale=inv_s2[:, 0:1]).then_inc(grav_e.sem, 1)

            def kt(pair, h):
                act.wait_ge(pb[h].full, pb[h].filled(pair, ("KT", h)))
                nc.scalar.activation(kt_h[:, h, :, :], pb[h].t[:].rearrange("p (t n) -> p t n", t=NT),
                                     ACT.Copy).then_inc(kt_hi.sem, 1)

            def rstd_of(s, chain, pair, key, h):
                act.wait_ge(var_known[s].sem, var_known[s].after(pair, key))
                chain.link(act, nc.scalar.activation(log_var[:, s, h, :], mean_var[:, s, h, :, 1], ACT.Ln, bias=eps_col[:, 0:1]))
                nc.scalar.activation(rstd[:, s, h, :], log_var[:, s, h, :], ACT.Exp, scale=-0.5).then_inc(rstd_known[s].sem, 1)

            def kv(pair, h):
                rstd_of(0, act_f, pair, ("KV", h), h)

            def x_split(s, pair, key, h, src):
                act.wait_ge(normed[s].sem, normed[s].after(pair, key))
                nc.scalar.activation(x_h[:, NT * h:NT * h + NT, :], src[:, NT * h:NT * h + NT, :],
                                     ACT.Copy).then_inc(x_hi[s].sem, 1)

            def kvn(pair, h):
                if not first(pair):
                    act.wait_ge(ub[1].full, ub[1].filled(pair - 1, ("L3", h)))
                x_split(0, pair, ("KVN", h), h, x1)

            def y(pair, layer, h):
                for i in range(KD):
                    b = yb[i % 2]
                    act.wait_ge(b.full, b.filled(pair, ("Y", layer, h, i)))
                    if i == 0 and layer == 1:
                        act.wait_ge(ub[1].full, ub[1].filled(pair, ("U", 0, h)))
                    elif i == 0 and not first(pair):
                        act.wait_ge(ub[1].full, ub[1].filled(pair - 1, ("U", 1, h)))
                    nc.scalar.activation(y_h[:, h, i, :], b.t[:, 0:YW], ACT.Copy).then_inc(y_hi.sem, 1)

            def before_u(pair, layer, h):
                u_keys = [k for k in ORDER if k[0] == "U"]
                n = u_keys.index(("U", layer, h))
                if n > 0:
                    act.wait_ge(ub[1].full, ub[1].filled(pair, u_keys[n - 1]))
                elif not first(pair):
                    act.wait_ge(ub[1].full, ub[1].filled(pair - 1, u_keys[-1]))

            def qk_rows(pair, layer, h):
                act.wait_ge(q_max.sem, q_max.after(pair, ("QK", layer, h)))
                before_factors(pair, layer, h)
                act.wait_ge(yb[1].full, yb[1].filled(pair, ("QK", layer, h)))
                act_b.link(act, nc.scalar.activation(s_pos[:], yb[1].t[:], ACT.Relu, bias=qs[:, h, 0:1]))
                nc.scalar.activation(s_neg[:], yb[1].t[:], ACT.Relu, bias=qs[:, h, 1:2], scale=-1.0).then_inc(yb[1].free, 1)
                act.wait_ge(yb[1].free, yb[1].read(pair, ("QK", layer, h)))
                nc.scalar.activation(s_pos[:], s_pos[:], ACT.Exp, scale=-(1.0 - LEAK))
                nc.scalar.activation(s_neg[:], s_neg[:], ACT.Exp, scale=-(1.0 - LEAK))
                nc.scalar.activation(ab[:, h, 0, :], qs[:, h, 2:2 + KD], ACT.Exp)
                nc.scalar.activation(ab[:, h, 1, :], qs[:, h, 2:2 + KD], ACT.Exp, scale=LEAK).then_inc(factors.sem, 1)

            def before_factors(pair, layer, h):
                keys = [k for k in ORDER if k[0] == "ATT"]
                n = keys.index(("ATT", layer, h))
                if n > 0:
                    act.wait_ge(att_val.sem, att_val.after(pair, keys[n - 1]))
                elif not first(pair):
                    act.wait_ge(att_val.sem, att_val.after(pair - 1, keys[-1]))

            def att_split(pair, layer, h):
                before_u(pair, layer, h)
                for i in range(KD):
                    act.wait_ge(att_val.sem, att_val.after(pair, ("ATT", layer, h), i + 1))
                    nc.scalar.activation(att_h[:, i, :], att[:, i, :], ACT.Copy).then_inc(att_hi.sem, 1)

            def rd(pair, layer, h):
                act.wait_ge(yb[1].full, yb[1].filled(pair, ("RD", layer, h)))
                nc.scalar.activation(inv_den_bc[:], yb[1].t[:], ACT.Copy).then_inc(yb[1].free, 1)

            def res(pair, layer, h):
                for ot in range(NT):
                    act.wait_ge(ub[ot].free, ub[ot].read(pair, ("U", layer, h)))
                    nc.scalar.activation(u[:, ot, :], u[:, ot, :], ACT.Relu, bias=bm[:, layer, ot:ot + 1]).then_inc(relued.sem, 1)
                rstd_of(1, act_b, pair, ("RES", layer, h), h)

            def nrm(pair, layer, h):
                x_split(1, pair, ("NRM", layer, h), h, x2)

            def l3(pair, h):
                rstd_of(1, act_b, pair, ("L3", h), h)

            schedule(act, {"XT": xt_split, "ZL": project("ZL", z_h), "ZG": project("ZG", z_h), "V": project("V", v_h),
                           "GL": gl, "HB": hb, "KT": kt, "KV": kv, "KVN": kvn, "Y": y, "QK": qk_rows,
                           "ATT": att_split, "RD": rd, "RES": res, "NRM": nrm, "L3": l3}, ((act_f,), (act_b,)))

        @block.vector
        def _(dve):
            sub, mult, add, vmax, vmin = ALU.subtract, ALU.mult, ALU.add, ALU.max, ALU.min
            nc.vector.memset(eps_col[:], LN_EPS)
            dve.wait_ge(small_in, 16 * 8)
            nc.vector.memset(ones[:], 1.0).then_inc(setup_dve, 1)
            dve.wait_ge(w_in2, 16)
            dve.wait_ge(setup_act, 4)
            nc.vector.tensor_tensor(wl_l[:], att[:], f32(wl_h[:]), sub).then_inc(setup_dve, 1)
            nc.vector.tensor_scalar(tiny[:, 3:4], tiny[:, 2:3], 1.0, None, add).then_inc(setup_dve, 1)
            nc.vector.tensor_tensor(grav[:, 0, :, :], offdiag[:], offdiag[:], mult).then_inc(setup_dve, 1)
            nc.vector.tensor_tensor(aq_l[:], x_small_view(xt_in, NT, AQ), f32(aq_h[:]), sub).then_inc(setup_dve, 1)
            dve.wait_ge(setup_dve, 4)
            nc.vector.reciprocal(w_lang_col[:], tiny[:, 3:4]).then_inc(setup_dve, 1)
            for j in range(NT):
                d = offdiag[:, j, j * P:(j + 1) * P]
                own = lang[:, 0, j, 0:P]
                nc.vector.tensor_scalar(own, ident[:], -1.0, 1.0, mult, add).then_inc(setup_own, 1)
                dve.wait_ge(setup_own, 2 * j + 1)
                nc.vector.tensor_tensor(d, d, own, mult).then_inc(setup_own, 1)
            dve.wait_ge(setup_dve, 6)
            nc.vector.tensor_scalar(w_grav_col[:], w_lang_col[:], -1.0, 1.0, mult, add).then_inc(setup_own, 1)
            dve.wait_ge(setup_own, 5)
            for k in range(KD):
                dve.wait_ge(setup_act, 5 + k)
                mm = nc.vector.tensor_tensor(wv_l[:, k, :], [pb, gb][k // 2][k % 2].t[:], f32(wv_h[:, k, :]), sub)
            mm.then_inc(setup_dve, 1)
            dve.wait_ge(setup_act, 9)
            nc.vector.tensor_tensor(wg_l[:], att[:], f32(wg_h[:]), sub).then_inc(setup_dve, 1)
            dve.wait_ge(setup_act, 10)
            nc.vector.tensor_tensor(a2_l[:], grav[:, 0, :, :], f32(a2_h[:]), sub).then_inc(setup_dve, 1)
            dve.wait_ge(setup_dve, 9)

            def xt_split(pair, c):
                dve.wait_ge(xt_hi.sem, xt_hi.after(pair, ("XT", c)))
                k = slice(2 * c, 2 * c + 2)
                nc.vector.tensor_tensor(xt_l[:, k, :], xt_in[:], f32(xt_h[:, k, :]), sub).then_inc(xt_lo.sem, 1)

            def project(kind, dst_h, dst_l):
                def do(pair, e):
                    b = pb[e % 2]
                    dve.wait_ge(proj_hi.sem, proj_hi.after(pair, (kind, e)))
                    nc.vector.tensor_tensor(dst_l[:, e, :], b.t[:], f32(dst_h[:, e, :]), sub).then_inc(b.free, 1)
                return do

            def diagonal(b, h, to, scratch):
                for j in range(NT):
                    ins = nc.vector.scalar_tensor_tensor(scratch[:, h, j, 0:P], b.t[:, j * N + j * P:j * N + (j + 1) * P], 1.0,
                                                         ident[:], mult, mult, accum_out=cols[:, h, to, j:j + 1])
                dve_f.link(dve, ins)

            def gl(pair, h):
                b = gb[h]
                dve.wait_ge(b.full, b.filled(pair, ("GL", h)))
                if not first(pair):
                    dve.wait_ge(pb[h].full, pb[h].filled(pair - 1, ("KT", h)))
                diagonal(b, h, SS, lang)
                nc.vector.tensor_scalar(cols[:, h, SS, :], cols[:, h, SS, :], EPS * EPS, None, vmax).then_inc(lang_sq.sem, 1)
                nc.vector.scalar_tensor_tensor(lang[:, h, :, :], b.t[:].rearrange("p (t n) -> p t n", t=NT), 0.0, offdiag[:],
                                               vmax, mult).then_inc(b.free, 1)
                dve.wait_ge(b.free, b.read(pair, ("GL", h)))

            def row_factor(h, deg, to, weight):
                dve_f.link(dve, nc.vector.tensor_scalar(cols[:, h, deg, :], cols[:, h, deg, :], EPS, None, vmax))
                dve_f.link(dve, nc.vector.reciprocal(cols[:, h, to, :], cols[:, h, deg, :]))
                dve_f.link(dve, nc.vector.tensor_scalar(cols[:, h, to, :], cols[:, h, to, :], weight[:, 0:1], None, mult))

            def rb(pair, h):
                b = pb[h]
                dve.wait_ge(b.full, b.filled(pair, ("RB", h)))
                for j in range(NT):
                    ins = nc.vector.scalar_tensor_tensor(lang[:, h, j, :], lang[:, h, j, :], cols[:, h, R, j:j + 1], b.t[:, 0:N],
                                                         mult, mult, accum_out=cols[:, h, DEGL, j:j + 1])
                ins.then_inc(b.free, 1)
                dve.wait_ge(b.free, b.read(pair, ("RB", h)))
                row_factor(h, DEGL, CL, w_lang_col)

            def gg(pair, h):
                b = gb[h]
                dve.wait_ge(b.full, b.filled(pair, ("GG", h)))
                diagonal(b, h, SQ, grav)
                nc.vector.tensor_scalar(cols[:, h, HSQ, :], cols[:, h, SQ, :], 0.5, None, mult).then_inc(grav_hsq.sem, 1)

            def hb(pair, h):
                b = gb[h]
                dve.wait_ge(pb[h].free, pb[h].read(pair, ("HB", h)))
                dve.wait_ge(grav_hsq.sem, grav_hsq.after(pair, ("GG", h)))
                for j in range(NT):
                    ins = nc.vector.scalar_tensor_tensor(grav[:, h, j, :], b.t[:, j * N:(j + 1) * N], cols[:, h, HSQ, j:j + 1],
                                                         half_sq_bc[:, h, :], sub, sub)
                ins.then_inc(b.free, 1)
                dve.wait_ge(b.free, b.read(pair, ("GG", h)))
                nc.vector.tensor_scalar(grav[:, h, :, :], grav[:, h, :, :], 0.0, None, vmin).then_inc(grav_d.sem, 1)

            def eg(pair, h):
                dve.wait_ge(grav_e.sem, grav_e.after(pair, ("HB", h)))
                for j in range(NT):
                    ins = nc.vector.scalar_tensor_tensor(grav[:, h, j, :], grav[:, h, j, :], 1.0, offdiag[:, j, :], mult, mult,
                                                         accum_out=cols[:, h, DEGG, j:j + 1])
                dve_f.link(dve, ins)
                row_factor(h, DEGG, CG, w_grav_col)
                for j in range(NT):
                    ins = nc.vector.tensor_scalar(grav[:, h, j, :], grav[:, h, j, :], cols[:, h, CG, j:j + 1], None, mult)
                dve_f.link(dve, ins)
                for j in range(NT):
                    ins = nc.vector.scalar_tensor_tensor(lang[:, h, j, :], lang[:, h, j, :], cols[:, h, CL, j:j + 1],
                                                         grav[:, h, j, :], mult, add)
                ins.then_inc(graph.sem, 1)

            def kt(pair, h):
                dve.wait_ge(kt_hi.sem, kt_hi.after(pair, ("KT", h)))
                nc.vector.tensor_tensor(kt_l[:, h, :, :], pb[h].t[:].rearrange("p (t n) -> p t n", t=NT), f32(kt_h[:, h, :, :]),
                                        sub).then_inc(pb[h].free, 1)

            def normalise(s, pair, stat_key, key, h, x):
                dve.wait_ge(rstd_known[s].sem, rstd_known[s].after(pair, stat_key))
                for j in range(NT):
                    t = x[:, NT * h + j, :]
                    nc.vector.tensor_scalar(t, t, mean_var[:, s, h, j, 0:1], rstd[:, s, h, j:j + 1], sub,
                                            mult).then_inc(normed[s].sem, 1)

            def kv(pair, h):
                dve.wait_ge(x0_loaded[h], 16 * pair + 16)
                for j in range(NT):
                    b = (gb, pb)[h][j]
                    t = x1[:, NT * h + j, :]
                    dve.wait_ge(b.full, b.filled(pair, ("KV", h)))
                    nc.vector.tensor_tensor(t, b.t[:], t, add).then_inc(b.free, 1)
                    dve.wait_ge(b.free, b.read(pair, ("KV", h)))
                for j in range(NT):
                    ins = nc.vector.bn_stats(stats[:, 0, h, j, :], x1[:, NT * h + j, :])
                dve_f.link(dve, ins)
                dve_carrier()
                for j in range(NT):
                    ins = nc.vector.bn_aggr(mean_var[:, 0, h, j, :], stats[:, 0, h, j, :])
                ins.then_inc(var_known[0].sem, 1)

            def kvn(pair, h):
                normalise(0, pair, ("KV", h), ("KVN", h), h, x1)

            def y(pair, layer, h):
                for i in range(KD):
                    b = yb[i % 2]
                    dve.wait_ge(y_hi.sem, y_hi.after(pair, ("Y", layer, h), i + 1))
                    nc.vector.tensor_tensor(y_l[:, h, i, :], b.t[:, 0:YW], f32(y_h[:, h, i, :]), sub).then_inc(b.free, 1)
                for n in range(2):
                    dve.wait_ge(yb[n].free, yb[n].read(pair, ("Y", layer, h, n + 2)))
                c = q_cols(layer)
                nc.vector.tensor_tensor(qk[:, h, :, :], f32(y_h[:, h, :, c]), f32(y_l[:, h, :, c]), add).then_inc(qk_cols.sem, 1)

            def qk_rows(pair, layer, h):
                b = yb[0]
                dve.wait_ge(b.full, b.filled(pair, ("QK", layer, h)))
                nc.vector.reduce_max(qs[:, h, 0:1], b.t[:], AX_X).then_inc(b.free, 1)
                dve.wait_ge(b.free, b.read(pair, ("QK", layer, h)))
                nc.vector.tensor_scalar(qs[:, h, 1:2], qs[:, h, 0:1], -1.0, None, mult)
                nc.vector.tensor_scalar(qs[:, h, 2:2 + KD], qk[:, h, :, 0], qs[:, h, 0:1], None, sub).then_inc(q_max.sem, 1)

            def attention(pair, layer, h):
                key = ("ATT", layer, h)
                dve.wait_ge(factors.sem, factors.after(pair, ("QK", layer, h)))

                def value(i):
                    dve.wait_ge(att_low.sem, att_low.after(pair, key, i + 1))
                    nc.vector.scalar_tensor_tensor(att[:, i, :], s_neg[:], ab[:, h, 0, i:i + 1], att[:, i, :], mult,
                                                   vmax).then_inc(att_val.sem, 1)

                def low(i):
                    dve.wait_ge(att_hi.sem, att_hi.after(pair, key, i + 1))
                    nc.vector.tensor_tensor(att_l[:, i, :], att[:, i, :], f32(att_h[:, i, :]), sub).then_inc(att_lo.sem, 1)

                value(0)
                value(1)
                low(0)
                value(2)
                low(1)
                value(3)
                low(2)
                low(3)

            def den(pair, layer, h):
                b = yb[0]
                dve.wait_ge(b.full, b.filled(pair, ("DEN", layer, h)))
                nc.vector.reciprocal(inv_den[:], b.t[:, 0:KD]).then_inc(b.free, 1)

            def res(pair, layer, h):
                dve.wait_ge(yb[1].free, yb[1].read(pair, ("RD", layer, h)))
                for ot in range(NT):
                    b = ub[ot]
                    dve.wait_ge(b.full, b.filled(pair, ("U", layer, h)))
                    nc.vector.tensor_tensor(u[:, ot, :], b.t[:], inv_den_bc[:], mult).then_inc(b.free, 1)
                if layer == 0 and not first(pair):
                    dve.wait_ge(stored[h], 16 * pair)
                src = x1 if layer == 0 else x2
                for ot in range(NT):
                    dve.wait_ge(relued.sem, relued.after(pair, ("RES", layer, h), ot + 1))
                    nc.vector.tensor_tensor(x2[:, NT * h + ot, :], u[:, ot, :], src[:, NT * h + ot, :],
                                            add).then_inc(added.sem, 1)
                for j in range(NT):
                    dve.wait_ge(added.sem, added.after(pair, ("RES", layer, h), j + 1))
                    ins = nc.vector.bn_stats(stats[:, 1, h, j, :], x2[:, NT * h + j, :])
                dve_b.link(dve, ins)
                dve_carrier()
                for j in range(NT):
                    ins = nc.vector.bn_aggr(mean_var[:, 1, h, j, :], stats[:, 1, h, j, :])
                ins.then_inc(var_known[1].sem, 1)

            def nrm(pair, layer, h):
                normalise(1, pair, ("RES", layer, h), ("NRM", layer, h), h, x2)

            def l3(pair, h):
                for mt in range(NT):
                    b = ub[mt]
                    t = x2[:, NT * h + mt, :]
                    dve.wait_ge(b.full, b.filled(pair, ("L3", h)))
                    dve.wait_ge(biased.sem, biased.after(pair, ("L3", h), mt + 1))
                    nc.vector.tensor_tensor(t, b.t[:], t, add).then_inc(b.free, 1)
                    dve.wait_ge(b.free, b.read(pair, ("L3", h)))
                    ins = nc.vector.bn_stats(stats[:, 1, h, mt, :], t)
                dve_b.link(dve, ins)
                dve_carrier()
                for j in range(NT):
                    ins = nc.vector.bn_aggr(mean_var[:, 1, h, j, :], stats[:, 1, h, j, :])
                ins.then_inc(var_known[1].sem, 1)

            def l3n(pair, h):
                normalise(1, pair, ("L3", h), ("L3N", h), h, x2)

            schedule(dve, {"XT": xt_split, "ZL": project("ZL", z_h, z_l), "ZG": project("ZG", z_h, z_l),
                           "V": project("V", v_h, v_l), "GL": gl, "RB": rb, "GG": gg, "HB": hb, "EG": eg, "KT": kt,
                           "KV": kv, "KVN": kvn, "Y": y, "QK": qk_rows, "ATT": attention, "DEN": den, "RES": res,
                           "NRM": nrm, "L3": l3, "L3N": l3n}, ((dve_f,), (dve_b,)))

        @block.gpsimd
        def _(pool):
            def attention(pair, layer, h):
                key = ("ATT", layer, h)
                keys = [k for k in ORDER if k[0] == "ATT"]
                n = keys.index(key)
                pool.wait_ge(factors.sem, factors.after(pair, ("QK", layer, h)))
                if n > 0:
                    pool.wait_ge(att_lo.sem, att_lo.after(pair, keys[n - 1]))
                    pool.wait_ge(summed.sem, summed.after(pair, keys[n - 1]))
                elif not first(pair):
                    pool.wait_ge(att_lo.sem, att_lo.after(pair - 1, keys[-1]))
                    pool.wait_ge(summed.sem, summed.after(pair - 1, keys[-1]))
                else:
                    pool.wait_ge(setup_dve, 8)
                pool_carrier()
                for i in range(KD):
                    nc.gpsimd.tensor_scalar(att[:, i, :], s_pos[:], ab[:, h, 1, i:i + 1], 1.0, ALU.mult,
                                            ALU.mult).then_inc(att_low.sem, 1)
                if n > 0:
                    pool.wait_ge(yb[0].full, yb[0].filled(pair, ("DEN",) + keys[n - 1][1:]))
                elif not first(pair):
                    pool.wait_ge(yb[0].full, yb[0].filled(pair - 1, ("DEN",) + keys[-1][1:]))
                pool.wait_ge(att_val.sem, att_val.after(pair, key, 2))
                pool_b.link(pool, nc.gpsimd.tensor_tensor(den_sum[:], att[:, 0, :], att[:, 1, :], ALU.add))
                pool.wait_ge(att_val.sem, att_val.after(pair, key, 3))
                pool_b.link(pool, nc.gpsimd.tensor_tensor(den_sum[:], den_sum[:], att[:, 2, :], ALU.add))
                pool.wait_ge(att_val.sem, att_val.after(pair, key, 4))
                nc.gpsimd.tensor_tensor(den_sum[:], den_sum[:], att[:, 3, :], ALU.add).then_inc(summed.sem, 1)

            def low(s, pair, key, h, src):
                pool.wait_ge(x_hi[s].sem, x_hi[s].after(pair, key))
                for j in range(NT):
                    t = NT * h + j
                    nc.gpsimd.tensor_tensor(x_l[:, t, :], src[:, t, :], f32(x_h[:, t, :]),
                                            ALU.subtract).then_inc(x_lo[s].sem, 1)

            def kvn(pair, h):
                low(0, pair, ("KVN", h), h, x1)

            def nrm(pair, layer, h):
                low(1, pair, ("NRM", layer, h), h, x2)
                if layer == 1:
                    pool.wait_ge(x_lo[1].sem, x_lo[1].after(pair, ("NRM", 1, h)))
                    for j in range(NT):
                        t = x2[:, NT * h + j, :]
                        nc.gpsimd.tensor_tensor(t, t, bias_bc[:], ALU.add).then_inc(biased.sem, 1)

            schedule(pool, {"ATT": attention, "KVN": kvn, "NRM": nrm}, ((), (pool_b,)))


def x_small_view(t, a, b):
    return t[:].rearrange("p c n -> p (c n)")[:, 0:a * b].rearrange("p (a b) -> p a b", a=a)


def kernel(x, adj, L0_gnn_W_lang, L0_gnn_W_grav, L0_gnn_W_V, L0_gnn_W_O, L0_gnn_gate_logit, L0_gnn_log_sigma,
           L1_gnn_wq, L1_gnn_wk, L1_gnn_bm, L2_gnn_wq, L2_gnn_wk, L2_gnn_bm, L3_gnn_bias):
    import numpy as np
    import concourse.bacc as bacc
    from concourse.bass_utils import run_bass_kernel_spmd

    a = {k: np.asarray(v) for k, v in locals().items() if k not in ("np", "bacc", "run_bass_kernel_spmd")}
    B, N, D = a["x"].shape
    PAIRS, NT, KD = B // 2, N // P, D // P
    col = lambda v: np.ascontiguousarray(v.reshape(-1, P).T)
    adj_t = a["adj"].T
    arrays = {
        "xn": np.ascontiguousarray(a["x"].reshape(PAIRS, 2 * NT, P, D).transpose(0, 2, 1, 3)),
        "xt": np.ascontiguousarray(a["x"].reshape(PAIRS, 2 * N, KD, P).transpose(0, 3, 2, 1)),
        "adj": np.ascontiguousarray(a["adj"]),
        "adjq": np.ascontiguousarray(np.concatenate(
            [a["L1_gnn_wq"][:, None], a["L1_gnn_wk"][:, None], adj_t, a["L2_gnn_wq"][:, None], a["L2_gnn_wk"][:, None]], axis=1)),
        "w_l": np.ascontiguousarray(a["L0_gnn_W_lang"].T),
        "w_g": np.ascontiguousarray(a["L0_gnn_W_grav"].T),
        "w_v": np.ascontiguousarray(a["L0_gnn_W_V"]),
        "w_o": np.ascontiguousarray(a["L0_gnn_W_O"].T),
        "gate": np.ascontiguousarray(np.broadcast_to(a["L0_gnn_gate_logit"].reshape(1, 1), (P, 1))),
        "sigma": np.ascontiguousarray(np.broadcast_to(a["L0_gnn_log_sigma"].reshape(1, 1), (P, 1))),
        "bm1": col(a["L1_gnn_bm"]),
        "bm2": col(a["L2_gnn_bm"]),
        "bias3": np.ascontiguousarray(np.broadcast_to(a["L3_gnn_bias"][None, :], (P, D))),
        "ident": np.eye(P, dtype=np.float32),
    }
    nc = bacc.Bacc("TRN2", target_bir_lowering=False, num_devices=1, dynamic_dma_scratch_size=1024)
    args = [nc.dram_tensor(f"in_{k}", v.shape, mybir.dt.from_np(v.dtype), kind="ExternalInput").ap() for k, v in arrays.items()]
    args.append(nc.dram_tensor("out", (PAIRS, P, 2 * NT, D), F32, kind="ExternalOutput").ap())
    resnorm_kernel(nc, *args)
    r = run_bass_kernel_spmd(nc, [{f"in_{k}": v for k, v in arrays.items()}], core_ids=[0])
    got = r.results[0]["out"]
    return np.ascontiguousarray(got.transpose(0, 2, 1, 3)).reshape(B, N, D)
```

```python
from contextlib import ExitStack

import concourse.bass as bass
from concourse import mybir

F32 = mybir.dt.float32
F32R = mybir.dt.float32r
ALU = mybir.AluOpType
ACT = mybir.ActivationFunctionType
AX_X = mybir.AxisListType.X

P = 128
LEAK = 0.01
LN_EPS = 1e-5
EPS = 1e-8

ORDERS = {
    "PE": """
    ZL.0 ZL.1 Y.0.0 Y.0.1 QK.0.0 ZL.2 ZL.3 QK.0.1 U.0.0 V.0 DEN.0.0 RD.0.0 GL.0 V.1 U.0.1 DEN.0.1 V.2 RD.0.1
    Y.1.0 QK.1.0 GL.1 V.3 ZG.0 Y.1.1 ZG.1 QK.1.1 ZG.2 U.1.0 DEN.1.0 ZG.3 RD.1.0 GG.0 RB.1 HB.0 GG.1 RB.0 HB.1
    U.1.1 DEN.1.1 RD.1.1 L3.0 KT.0 KT.1 L3.1 KV.0 KV.1
    """,
    "ACT": """
    ZL.0 ZL.1 Y.0.0 Y.0.1 QK.0.0 ATT.0.0 ZL.2 ZL.3 QK.0.1 V.0 ATT.0.1 RD.0.0 RES.0.0 NRM.0.0 GL.0 V.1 V.2
    RD.0.1 Y.1.0 RES.0.1 NRM.0.1 QK.1.0 GL.1 V.3 ZG.0 Y.1.1 ATT.1.0 ZG.1 QK.1.1 ZG.2 ATT.1.1 ZG.3 RD.1.0
    RES.1.0 HB.0 NRM.1.0 HB.1 RD.1.1 RES.1.1 XT.0 NRM.1.1 L3.0 KT.0 XT.1 KT.1 L3.1 KV.0 KV.1 KVN.0 KVN.1
    """,
    "DVE": """
    ZL.0 ZL.1 Y.0.0 Y.0.1 QK.0.0 ATT.0.0 ZL.2 ZL.3 QK.0.1 V.0 DEN.0.0 ATT.0.1 RES.0.0 NRM.0.0 GL.0 V.1 DEN.0.1
    V.2 Y.1.0 RES.0.1 NRM.0.1 QK.1.0 GL.1 V.3 ZG.0 Y.1.1 ATT.1.0 ZG.1 QK.1.1 ZG.2 DEN.1.0 ATT.1.1 ZG.3 RES.1.0
    GG.0 RB.1 HB.0 GG.1 NRM.1.0 RB.0 HB.1 EG.0 DEN.1.1 RES.1.1 NRM.1.1 EG.1 L3.0 KT.0 KT.1 L3.1 KV.0 KV.1
    KVN.0 KVN.1 L3N.0 L3N.1
    """,
    "POOL": """
    ATT.0.0 ATT.0.1 RES.0.0 NRM.0.0 RES.0.1 NRM.0.1 ATT.1.0 ATT.1.1 RES.1.0 NRM.1.0 RES.1.1 XT.0 NRM.1.1 XT.1
    KVN.0 KVN.1
    """,
    "SP": """
    RES.0.0 RES.0.1 XT.0 XT.1 L3N.0 L3N.1
    """,
}
ORDERS = {e: [(t[0],) + tuple(int(x) for x in t[1:]) for t in (w.split(".") for w in text.split())]
          for e, text in ORDERS.items()}
FRONT = {"XT", "ZL", "ZG", "V", "GL", "GG", "RB", "HB", "EG", "KT", "KV", "KVN"}


class Signal:

    def __init__(self, sem, engine, stages, each=1, step=1):
        self.sem, self.each, self.step = sem, each, step
        self.at = {key: n for n, key in enumerate(k for k in ORDERS[engine] if k[0] in stages or k[:2] in stages)}
        self.per_pair = len(self.at) * each

    def after(self, pair, key, k=None):
        k = self.each if k is None else k
        return (pair * self.per_pair + self.at[key] * self.each + k) * self.step


class Bank:

    def __init__(self, tensor, full, free, uses):
        self.t, self.full, self.free = tensor, full, free
        self.at = {key: n for n, key in enumerate(uses)}
        self.n = len(uses)

    def filled(self, pair, key):
        return pair * self.n + self.at[key] + 1

    read = filled

    def before(self, pair, key):
        return pair * self.n + self.at[key]


class Chain:

    def __init__(self, sem):
        self.sem, self.k, self.n, self.pair = sem, 0, None, 0

    def begin(self, pair):
        if self.n is None and not (isinstance(pair, int) and pair == 0):
            self.n = self.k
        self.pair, self.k = pair, 0

    def link(self, eng, ins):
        ins.then_inc(self.sem, 1)
        self.k += 1
        base = 0 if self.n is None else self.pair * self.n
        eng.wait_ge(self.sem, base + self.k)


def uses_of(bank):
    kind, n = bank
    out = []
    for key in ORDERS["PE"]:
        s, a = key[0], key[1:]
        if kind == "P":
            if s in ("ZL", "ZG", "V") and a[0] % 2 == n:
                out.append(key)
            if s in ("RB", "HB", "KT") and a[0] == n:
                out.append(key)
            if s == "KV" and a[0] == 1:
                out.append(key)
        if kind == "G":
            if s in ("GL", "GG") and a[0] == n:
                out.append(key)
            if s == "KV" and a[0] == 0:
                out.append(key)
        if kind == "Y":
            if s == "Y":
                out += [key + (n,), key + (n + 2,)]
            if s == "QK" or (s == "DEN" and n == 0) or (s == "RD" and n == 1):
                out.append(key)
        if kind == "U" and s in ("U", "L3"):
            out.append(key)
    return out


def resnorm_kernel(nc, xn, xt, adj, adjq, w_l, w_g, w_v, w_o, gate, sigma, bm1, bm2, bias3, ident_in, out):
    PAIRS = xn.shape[0]
    D = xn.shape[3]
    KD = D // P
    N = adj.shape[0]
    NT = N // P
    AQ = adjq.shape[1]
    YW = N + 2

    with ExitStack() as ctx:
        def sb(name, shape, dt=F32):
            return ctx.enter_context(nc.sbuf_tensor(name, shape, dt))

        def sem(name):
            return ctx.enter_context(nc.semaphore(name))

        wl_h, wl_l = sb("wl_h", [P, KD, D], F32R), sb("wl_l", [P, KD, D], F32R)
        wg_h, wg_l = sb("wg_h", [P, KD, D], F32R), sb("wg_l", [P, KD, D], F32R)
        wv_h, wv_l = sb("wv_h", [P, KD, D], F32R), sb("wv_l", [P, KD, D], F32R)
        aq_h, aq_l = sb("aq_h", [P, NT, AQ], F32R), sb("aq_l", [P, NT, AQ], F32R)
        a2_h, a2_l = sb("a2_h", [P, NT, N], F32R), sb("a2_l", [P, NT, N], F32R)
        offdiag = sb("offdiag", [P, NT, N])
        ident = sb("ident", [P, P])
        ones = sb("ones", [P, 1])
        bias_bc = sb("bias_bc", [P, D])
        bm = sb("bm", [P, 2, NT])
        w_lang_col, w_grav_col = sb("w_lang_col", [P, 1]), sb("w_grav_col", [P, 1])
        inv_s2 = sb("inv_s2", [P, 1])
        eps_col = sb("eps_col", [P, 1])
        tiny = sb("tiny", [P, 4])
        carrier = sb("carrier", [P, 1])

        xt_in = sb("xt_in", [P, 2, D])
        xt_h, xt_l = sb("xt_h", [P, KD, D], F32R), sb("xt_l", [P, KD, D], F32R)
        z_h, z_l = sb("z_h", [P, KD, D], F32R), sb("z_l", [P, KD, D], F32R)
        v_h, v_l = sb("v_h", [P, KD, D], F32R), sb("v_l", [P, KD, D], F32R)
        lang = sb("lang", [P, 2, NT, N])
        grav = sb("grav", [P, 2, NT, N])
        half_sq_bc = sb("half_sq_bc", [P, 2, N])
        kt_h, kt_l = sb("kt_h", [P, 2, NT, N], F32R), sb("kt_l", [P, 2, NT, N], F32R)
        cols = sb("cols", [P, 2, 12, NT])
        SS, LNS, R, SQ, HSQ, DEGL, CL, DEGG, CG = range(9)

        x1 = sb("x1", [P, 2 * NT, D])
        x2 = sb("x2", [P, 2 * NT, D])
        x_h, x_l = sb("x_h", [P, 2 * NT, D], F32R), sb("x_l", [P, 2 * NT, D], F32R)
        stats = sb("stats", [P, 2, 2, NT, 6])
        mean_var = sb("mean_var", [P, 2, 2, NT, 2])
        log_var = sb("log_var", [P, 2, 2, NT])
        rstd = sb("rstd", [P, 2, 2, NT])

        y_h, y_l = sb("y_h", [P, 2, KD, YW], F32R), sb("y_l", [P, 2, KD, YW], F32R)
        qk = sb("qk", [P, 2, KD, 2])
        qs = sb("qs", [P, 2, 2 + KD])
        ab = sb("ab", [P, 2, 2, KD])
        s_neg, s_pos = sb("s_neg", [P, D]), sb("s_pos", [P, D])
        att = sb("att", [P, KD, D])
        att_h, att_l = sb("att_h", [P, KD, D], F32R), sb("att_l", [P, KD, D], F32R)
        den_sum = sb("den_sum", [P, D])
        inv_den = sb("inv_den", [P, KD])
        inv_den_bc = sb("inv_den_bc", [P, D])
        u = sb("u", [P, NT, D])

        def bank(kind, n):
            name = f"{kind}{n}".lower()
            t = ctx.enter_context(nc.psum_tensor("bank_" + name, [P, D], F32))
            return Bank(t, sem(name + "_full"), sem(name + "_free"), uses_of((kind, n)))

        pb = [bank("P", 0), bank("P", 1)]
        gb = [bank("G", 0), bank("G", 1)]
        yb = [bank("Y", 0), bank("Y", 1)]
        ub = [bank("U", 0), bank("U", 1)]

        w_in, setup_wov, setup_act, setup_dve = sem("w_in"), sem("setup_wov"), sem("setup_act"), sem("setup_dve")
        w_in2 = sem("w_in2")
        small_in, setup_own = sem("small_in"), sem("setup_own")
        xt_loaded = Signal(sem("xt_loaded"), "SP", ("XT",), step=16)
        x0_loaded = [sem("x0_loaded_0"), sem("x0_loaded_1")]
        stored = [sem("stored_0"), sem("stored_1")]
        xt_hi = Signal(sem("xt_hi"), "ACT", ("XT",))
        xt_lo = Signal(sem("xt_lo"), "POOL", ("XT",))
        proj_hi = Signal(sem("proj_hi"), "ACT", ("ZL", "ZG", "V"))
        lang_sq = Signal(sem("lang_sq"), "DVE", ("GL",))
        lang_r = Signal(sem("lang_r"), "ACT", ("GL",))
        grav_hsq = Signal(sem("grav_hsq"), "DVE", ("GG",))
        grav_d = Signal(sem("grav_d"), "DVE", ("HB",))
        grav_e = Signal(sem("grav_e"), "ACT", ("HB",))
        graph = Signal(sem("graph"), "DVE", ("EG",))
        kt_hi = Signal(sem("kt_hi"), "ACT", ("KT",))
        added = [Signal(sem("added_0"), "POOL", ("RES",)), Signal(sem("added_1"), "DVE", ("RES",))]
        var_known = [Signal(sem("f_var"), "DVE", ("KV",)), Signal(sem("b_var"), "DVE", ("RES", "L3"))]
        rstd_known = [Signal(sem("f_rstd"), "ACT", ("KV",)), Signal(sem("b_rstd"), "ACT", ("RES", "L3"))]
        normed = [Signal(sem("f_normed"), "DVE", ("KVN",), 2), Signal(sem("b_normed"), "DVE", ("NRM", "L3N"), 2)]
        x_hi = [Signal(sem("f_x_hi"), "ACT", ("KVN",), 2), Signal(sem("b_x_hi"), "ACT", ("NRM",), 2)]
        x_lo = [[Signal(sem("f_x_lo_0"), "POOL", ("KVN",)), Signal(sem("f_x_lo_1"), "DVE", ("KVN",))],
                [Signal(sem("b_x_lo_0"), "POOL", ("NRM",)), Signal(sem("b_x_lo_1"), "DVE", ("NRM",))]]
        biased = Signal(sem("biased"), "POOL", (("NRM", 1),), 2)
        y_hi = Signal(sem("y_hi"), "ACT", ("Y",), 4)
        qk_cols = Signal(sem("qk_cols"), "DVE", ("Y",))
        q_max = Signal(sem("q_max"), "DVE", ("QK",))
        factors = Signal(sem("factors"), "ACT", ("QK",))
        att_low = Signal(sem("att_low"), "ACT", ("ATT",), 4)
        att_val = Signal(sem("att_val"), "DVE", ("ATT",), 4)
        att_hi = Signal(sem("att_hi"), "ACT", ("ATT",), 4)
        att_lo = Signal(sem("att_lo"), "DVE", ("ATT",), 4)
        summed = Signal(sem("summed"), "POOL", ("ATT",))
        relued = Signal(sem("relued"), "ACT", ("RES",), 2)
        dve_f, dve_b = Chain(sem("dve_f")), Chain(sem("dve_b"))
        act_f, act_b = Chain(sem("act_f")), Chain(sem("act_b"))
        pool_b = Chain(sem("pool_b"))

        def f32(ap):
            return ap.bitcast(F32)

        def y_cols(layer, ot):
            at = (2 if layer == 0 else 0) + ot * P
            return slice(at, at + P)

        def q_cols(layer):
            return slice(0, 2) if layer == 0 else slice(N, N + 2)

        def schedule(eng, order, stages, chains):
            fchains, bchains = chains

            def one(front, back, ahead=True):
                for c in fchains:
                    if front is not None:
                        c.begin(front)
                for c in bchains:
                    if back is not None:
                        c.begin(back)
                for key in ORDERS[order]:
                    do = stages[key[0]]
                    if key[0] == "XT":
                        if front is not None and ahead:
                            do(front + 1, *key[1:])
                    elif key[0] in FRONT:
                        if front is not None:
                            do(front, *key[1:])
                    elif back is not None:
                        do(back, *key[1:])

            if "XT" in stages:
                stages["XT"](0, 0)
                stages["XT"](0, 1)
            one(0, None)
            one(1, 0)
            with eng.Fori(2, PAIRS - 1) as i:
                one(i, i - 1)
            one(PAIRS - 1, PAIRS - 2, ahead=False)
            one(None, PAIRS - 1)

        def first(pair):
            return isinstance(pair, int) and pair == 0

        def dve_carrier():
            nc.vector.memset(carrier[:, 0:1], 0.0)

        block = ctx.enter_context(nc.Block())

        @block.sync
        def _(sp):
            for n, (t, src) in enumerate(((ident, ident_in), (offdiag, adj.rearrange("(t p) m -> p t m", p=P)),
                                          (bias_bc, bias3), (bm[:, 0, :], bm1), (bm[:, 1, :], bm2),
                                          (tiny[:, 0:1], gate), (tiny[:, 1:2], sigma),
                                          (x_small_view(xt_in, NT, AQ), adjq.rearrange("(t p) m -> p t m", p=P)))):
                sp.dma_start(t if n in (3, 4, 5, 6, 7) else t[:], src).then_inc(small_in, 16)
            sp.dma_start(x1[:], w_o.rearrange("(t p) m -> p t m", p=P)).then_inc(w_in, 16)
            sp.dma_start(x2[:], w_v.rearrange("(t p) m -> p t m", p=P)).then_inc(w_in, 16)
            sp.dma_start(att[:], w_l.rearrange("(t p) m -> p t m", p=P)).then_inc(w_in2, 16)
            sp.wait_ge(setup_dve, 2)
            sp.dma_start(att[:], w_g.rearrange("(t p) m -> p t m", p=P)).then_inc(w_in2, 16)

            def load_xt(pair, c):
                if c == 1:
                    sp.wait_ge(xt_lo.sem, xt_lo.after(pair, ("XT", 0)))
                elif not first(pair):
                    sp.wait_ge(xt_lo.sem, xt_lo.after(pair - 1, ("XT", 1)))
                else:
                    sp.wait_ge(setup_dve, 5)
                sp.dma_start(xt_in[:], xt[pair, :, 2 * c:2 * c + 2, :]).then_inc(xt_loaded.sem, 16)

            def load_x0(pair, h):
                if first(pair):
                    sp.wait_ge(setup_wov, 4)
                else:
                    for a in added:
                        sp.wait_ge(a.sem, a.after(pair - 1, ("RES", 0, h)))
                sp.dma_start(x1[:, NT * h:NT * h + NT, :], xn[pair, :, NT * h:NT * h + NT, :]).then_inc(x0_loaded[h], 16)

            def store(pair, h):
                sp.wait_ge(normed[1].sem, normed[1].after(pair, ("L3N", h)))
                sp.dma_start(out[pair, :, NT * h:NT * h + NT, :], x2[:, NT * h:NT * h + NT, :]).then_inc(stored[h], 16)

            load_xt(0, 0)
            load_x0(0, 0)
            load_x0(0, 1)
            load_xt(0, 1)
            load_xt(1, 0)
            load_xt(1, 1)

            def one(front, back, ahead):
                for key in ORDERS["SP"]:
                    if key[0] == "RES" and front is not None:
                        load_x0(front, key[2])
                    if key[0] == "XT" and ahead:
                        load_xt(front + 1, key[1])
                    if key[0] == "L3N" and back is not None:
                        store(back, key[1])

            one(1, 0, True)
            with sp.Fori(2, PAIRS - 1) as i:
                one(i, i - 1, True)
            one(PAIRS - 1, PAIRS - 2, False)
            one(None, PAIRS - 1, False)
            for h in range(2):
                sp.wait_ge(stored[h], 16 * PAIRS)

        @block.tensor
        def _(pe):
            def split_product(outap, pairs, start, stop):
                last = None
                n = 3 * len(pairs)
                m = 0
                for sh, sl, mh, ml in pairs:
                    for a, b in ((sh, mh), (sh, ml), (sl, mh)):
                        last = pe.matmul(outap, a, b, start=start and m == 0, stop=stop and m == n - 1)
                        m += 1
                return last

            def take(b, pair, key):
                if not (first(pair) and b.at[key] == 0):
                    pe.wait_ge(b.free, b.before(pair, key))

            pe.wait_ge(w_in, 32)
            for k in range(KD):
                for e in range(KD):
                    mm = pe.matmul([pb, gb][k // 2][k % 2].t[:], x2[:, e, k * P:(k + 1) * P], x1[:, e, :],
                                   start=e == 0, stop=e == KD - 1)
                mm.then_inc(setup_wov, 1)
            pe.wait_ge(setup_dve, 9)

            def project(kind, weights_h, weights_l):
                def do(pair, e):
                    key = (kind, e)
                    b = pb[e % 2]
                    take(b, pair, key)
                    if key == ("ZL", 0):
                        pe.wait_ge(xt_lo.sem, xt_lo.after(pair, ("XT", 1)))
                    c = slice(e * P, (e + 1) * P)
                    if kind == "V":
                        ops = [(xt_h[:, k, c], xt_l[:, k, c], weights_h[:, k, :], weights_l[:, k, :]) for k in range(KD)]
                    else:
                        ops = [(weights_h[:, k, c], weights_l[:, k, c], xt_h[:, k, :], xt_l[:, k, :]) for k in range(KD)]
                    split_product(b.t[:], ops, True, True).then_inc(b.full, 1)
                return do

            def gram(kind, z):
                def do(pair, h):
                    key = (kind, h)
                    b = gb[h]
                    take(b, pair, key)
                    for n in (2, 3):
                        pe.wait_ge(pb[n % 2].free, pb[n % 2].read(pair, (z, n)))
                    m = slice(h * N, (h + 1) * N)
                    for j in range(NT):
                        c = slice(h * N + j * P, h * N + (j + 1) * P)
                        mm = split_product(b.t[:, j * N:(j + 1) * N],
                                           [(z_h[:, k, c], z_l[:, k, c], z_h[:, k, m], z_l[:, k, m]) for k in range(KD)],
                                           True, True)
                    mm.then_inc(b.full, 1)
                return do

            def spread(outap, col):
                return pe.transpose(outap, col.broadcast_to([P, P]), ident[:])

            def rb(pair, h):
                take(pb[h], pair, ("RB", h))
                pe.wait_ge(lang_r.sem, lang_r.after(pair, ("GL", h)))
                for j in range(NT):
                    mm = spread(pb[h].t[:, j * P:(j + 1) * P], cols[:, h, R, j:j + 1])
                mm.then_inc(pb[h].full, 1)

            def hb(pair, h):
                take(pb[h], pair, ("HB", h))
                pe.wait_ge(grav_hsq.sem, grav_hsq.after(pair, ("GG", h)))
                for j in range(NT):
                    mm = spread(pb[h].t[:, j * P:(j + 1) * P], cols[:, h, HSQ, j:j + 1])
                mm.then_inc(pb[h].full, 1)

            def kt(pair, h):
                take(pb[h], pair, ("KT", h))
                pe.wait_ge(graph.sem, graph.after(pair, ("EG", h)))
                for mt in range(NT):
                    for j in range(NT):
                        mm = pe.transpose(pb[h].t[:, mt * N + j * P:mt * N + (j + 1) * P],
                                          lang[:, h, j, mt * P:(mt + 1) * P], ident[:])
                mm.then_inc(pb[h].full, 1)

            def kv(pair, h):
                pe.wait_ge(pb[h].free, pb[h].read(pair, ("KT", h)))
                for j in range(NT):
                    b = (gb, pb)[h][j]
                    take(b, pair, ("KV", h))
                    c = slice(j * P, (j + 1) * P)
                    split_product(b.t[:], [(kt_h[:, h, mt, c], kt_l[:, h, mt, c], v_h[:, NT * h + mt, :],
                                            v_l[:, NT * h + mt, :]) for mt in range(NT)],
                                  True, True).then_inc(b.full, 1)

            def y(pair, layer, h):
                for j in range(NT):
                    low, key = (x_lo[0][j], ("KVN", h)) if layer == 0 else (x_lo[1][j], ("NRM", 0, h))
                    pe.wait_ge(low.sem, low.after(pair, key))
                m = slice(0, YW) if layer == 0 else slice(2, 2 + YW)
                for i in range(KD):
                    b = yb[i % 2]
                    take(b, pair, ("Y", layer, h, i))
                    c = slice(i * P, (i + 1) * P)
                    split_product(b.t[:, 0:YW], [(x_h[:, NT * h + t, c], x_l[:, NT * h + t, c], aq_h[:, t, m], aq_l[:, t, m])
                                                 for t in range(NT)], True, True).then_inc(b.full, 1)

            def qk_rows(pair, layer, h):
                key = ("QK", layer, h)
                pe.wait_ge(qk_cols.sem, qk_cols.after(pair, ("Y", layer, h)))
                for w in range(2):
                    take(yb[w], pair, key)
                    for i in range(KD):
                        mm = spread(yb[w].t[:, i * P:(i + 1) * P], qk[:, h, i, w:w + 1])
                    mm.then_inc(yb[w].full, 1)

            def apply(pair, layer, h):
                for i in range(KD):
                    pe.wait_ge(att_lo.sem, att_lo.after(pair, ("ATT", layer, h), i + 1))
                    for ot in range(NT):
                        if i == 0:
                            take(ub[ot], pair, ("U", layer, h))
                        c = y_cols(layer, ot)
                        mm = split_product(ub[ot].t[:], [(y_h[:, h, i, c], y_l[:, h, i, c], att_h[:, i, :], att_l[:, i, :])],
                                           i == 0, i == KD - 1)
                        if i == KD - 1:
                            mm.then_inc(ub[ot].full, 1)

            def den(pair, layer, h):
                take(yb[0], pair, ("DEN", layer, h))
                pe.wait_ge(summed.sem, summed.after(pair, ("ATT", layer, h)))
                for i in range(KD):
                    mm = pe.matmul(yb[0].t[:, i:i + 1], den_sum[:, i * P:(i + 1) * P], ones[:, 0:1], start=True, stop=True)
                mm.then_inc(yb[0].full, 1)

            def rd(pair, layer, h):
                take(yb[1], pair, ("RD", layer, h))
                pe.wait_ge(yb[0].free, yb[0].read(pair, ("DEN", layer, h)))
                for i in range(KD):
                    mm = spread(yb[1].t[:, i * P:(i + 1) * P], inv_den[:, i:i + 1])
                mm.then_inc(yb[1].full, 1)

            def l3(pair, h):
                for low in x_lo[1]:
                    pe.wait_ge(low.sem, low.after(pair, ("NRM", 1, h)))
                for mt in range(NT):
                    take(ub[mt], pair, ("L3", h))
                    c = slice(mt * P, (mt + 1) * P)
                    split_product(ub[mt].t[:], [(a2_h[:, t, c], a2_l[:, t, c], x_h[:, NT * h + t, :], x_l[:, NT * h + t, :])
                                                for t in range(NT)], True, True).then_inc(ub[mt].full, 1)

            schedule(pe, "PE", {"ZL": project("ZL", wl_h, wl_l), "ZG": project("ZG", wg_h, wg_l), "V": project("V", wv_h, wv_l),
                          "GL": gram("GL", "ZL"), "GG": gram("GG", "ZG"), "RB": rb, "HB": hb, "KT": kt, "KV": kv,
                          "Y": y, "QK": qk_rows, "U": apply, "DEN": den, "RD": rd, "L3": l3}, ((), ()))

        @block.scalar
        def _(act):
            nc.scalar.preload_act_table_set("natural_log_exp_and_others")
            act.wait_ge(small_in, 16 * 8)
            nc.scalar.activation(aq_h[:], x_small_view(xt_in, NT, AQ), ACT.Copy).then_inc(setup_act, 1)
            nc.scalar.activation(tiny[:, 2:3], tiny[:, 0:1], ACT.Exp, scale=-1.0).then_inc(setup_act, 1)
            nc.scalar.activation(inv_s2[:], tiny[:, 1:2], ACT.Exp, scale=-2.0).then_inc(setup_act, 1)
            act.wait_ge(w_in2, 16)
            nc.scalar.activation(wl_h[:], att[:], ACT.Copy).then_inc(setup_act, 1)
            for k in range(KD):
                act.wait_ge(setup_wov, k + 1)
                nc.scalar.activation(wv_h[:, k, :], [pb, gb][k // 2][k % 2].t[:], ACT.Copy).then_inc(setup_act, 1)
            act.wait_ge(w_in2, 32)
            nc.scalar.activation(wg_h[:], att[:], ACT.Copy).then_inc(setup_act, 1)
            act.wait_ge(setup_dve, 4)
            nc.scalar.activation(a2_h[:], grav[:, 0, :, :], ACT.Copy).then_inc(setup_act, 1)

            def xt_split(pair, c):
                act.wait_ge(xt_loaded.sem, xt_loaded.after(pair, ("XT", c)))
                if not first(pair):
                    last = max((("ZL", 3), ("ZG", 3), ("V", 3)), key=ORDERS["PE"].index)
                    act.wait_ge(pb[1].full, pb[1].filled(pair - 1, last))
                nc.scalar.activation(xt_h[:, 2 * c:2 * c + 2, :], xt_in[:], ACT.Copy).then_inc(xt_hi.sem, 1)

            def project(kind, dst):
                def do(pair, e):
                    b = pb[e % 2]
                    act.wait_ge(b.full, b.filled(pair, (kind, e)))
                    if kind == "ZG":
                        act.wait_ge(gb[1].full, gb[1].filled(pair, ("GL", 1)))
                    elif kind == "ZL" and not first(pair):
                        act.wait_ge(gb[1].full, gb[1].filled(pair - 1, ("GG", 1)))
                    elif kind == "V" and not first(pair):
                        act.wait_ge(pb[1].full, pb[1].filled(pair - 1, ("KV", 1)))
                    nc.scalar.activation(dst[:, e, :], b.t[:], ACT.Copy).then_inc(proj_hi.sem, 1)
                return do

            def gl(pair, h):
                act.wait_ge(lang_sq.sem, lang_sq.after(pair, ("GL", h)))
                act_f.link(act, nc.scalar.activation(cols[:, h, LNS, :], cols[:, h, SS, :], ACT.Ln))
                nc.scalar.activation(cols[:, h, R, :], cols[:, h, LNS, :], ACT.Exp, scale=-0.5).then_inc(lang_r.sem, 1)

            def hb(pair, h):
                act.wait_ge(pb[h].full, pb[h].filled(pair, ("HB", h)))
                nc.scalar.activation(half_sq_bc[:, h, :], pb[h].t[:, 0:N], ACT.Copy).then_inc(pb[h].free, 1)
                act.wait_ge(grav_d.sem, grav_d.after(pair, ("HB", h)))
                nc.scalar.activation(grav[:, h, :, :], grav[:, h, :, :], ACT.Exp, scale=inv_s2[:, 0:1]).then_inc(grav_e.sem, 1)

            def kt(pair, h):
                act.wait_ge(pb[h].full, pb[h].filled(pair, ("KT", h)))
                nc.scalar.activation(kt_h[:, h, :, :], pb[h].t[:].rearrange("p (t n) -> p t n", t=NT),
                                     ACT.Copy).then_inc(kt_hi.sem, 1)

            def rstd_of(s, chain, pair, key, h):
                act.wait_ge(var_known[s].sem, var_known[s].after(pair, key))
                chain.link(act, nc.scalar.activation(log_var[:, s, h, :], mean_var[:, s, h, :, 1], ACT.Ln, bias=eps_col[:, 0:1]))
                nc.scalar.activation(rstd[:, s, h, :], log_var[:, s, h, :], ACT.Exp, scale=-0.5).then_inc(rstd_known[s].sem, 1)

            def kv(pair, h):
                rstd_of(0, act_f, pair, ("KV", h), h)

            def x_split(s, pair, key, h, src):
                for j in range(NT):
                    act.wait_ge(normed[s].sem, normed[s].after(pair, key, j + 1))
                    nc.scalar.activation(x_h[:, NT * h + j, :], src[:, NT * h + j, :], ACT.Copy).then_inc(x_hi[s].sem, 1)

            def kvn(pair, h):
                if not first(pair):
                    act.wait_ge(ub[1].full, ub[1].filled(pair - 1, ("L3", h)))
                x_split(0, pair, ("KVN", h), h, x1)

            def y(pair, layer, h):
                for i in range(KD):
                    b = yb[i % 2]
                    act.wait_ge(b.full, b.filled(pair, ("Y", layer, h, i)))
                    if i == 0 and layer == 1:
                        act.wait_ge(ub[1].full, ub[1].filled(pair, ("U", 0, h)))
                    elif i == 0 and not first(pair):
                        act.wait_ge(ub[1].full, ub[1].filled(pair - 1, ("U", 1, h)))
                    nc.scalar.activation(y_h[:, h, i, :], b.t[:, 0:YW], ACT.Copy).then_inc(y_hi.sem, 1)

            def before_u(pair, layer, h):
                u_keys = [k for k in ORDERS["PE"] if k[0] == "U"]
                n = u_keys.index(("U", layer, h))
                if n > 0:
                    act.wait_ge(ub[1].full, ub[1].filled(pair, u_keys[n - 1]))
                elif not first(pair):
                    act.wait_ge(ub[1].full, ub[1].filled(pair - 1, u_keys[-1]))

            def qk_rows(pair, layer, h):
                act.wait_ge(q_max.sem, q_max.after(pair, ("QK", layer, h)))
                before_factors(pair, layer, h)
                act.wait_ge(yb[1].full, yb[1].filled(pair, ("QK", layer, h)))
                act_b.link(act, nc.scalar.activation(s_pos[:], yb[1].t[:], ACT.Relu, bias=qs[:, h, 0:1]))
                nc.scalar.activation(s_neg[:], yb[1].t[:], ACT.Relu, bias=qs[:, h, 1:2], scale=-1.0).then_inc(yb[1].free, 1)
                act.wait_ge(yb[1].free, yb[1].read(pair, ("QK", layer, h)))
                nc.scalar.activation(s_pos[:], s_pos[:], ACT.Exp, scale=-(1.0 - LEAK))
                nc.scalar.activation(s_neg[:], s_neg[:], ACT.Exp, scale=-(1.0 - LEAK))
                nc.scalar.activation(ab[:, h, 0, :], qs[:, h, 2:2 + KD], ACT.Exp)
                nc.scalar.activation(ab[:, h, 1, :], qs[:, h, 2:2 + KD], ACT.Exp, scale=LEAK).then_inc(factors.sem, 1)

            def before_factors(pair, layer, h):
                keys = [k for k in ORDERS["DVE"] if k[0] == "ATT"]
                n = keys.index(("ATT", layer, h))
                if n > 0:
                    act.wait_ge(att_val.sem, att_val.after(pair, keys[n - 1]))
                elif not first(pair):
                    act.wait_ge(att_val.sem, att_val.after(pair - 1, keys[-1]))

            def att_split(pair, layer, h):
                before_u(pair, layer, h)
                keys = [k for k in ORDERS["DVE"] if k[0] == "ATT"]
                n = keys.index(("ATT", layer, h))
                if n > 0:
                    act.wait_ge(att_lo.sem, att_lo.after(pair, keys[n - 1]))
                    act.wait_ge(summed.sem, summed.after(pair, keys[n - 1]))
                elif not first(pair):
                    act.wait_ge(att_lo.sem, att_lo.after(pair - 1, keys[-1]))
                    act.wait_ge(summed.sem, summed.after(pair - 1, keys[-1]))
                else:
                    act.wait_ge(setup_dve, 8)
                act.wait_ge(factors.sem, factors.after(pair, ("QK", layer, h)))
                for i in range(KD):
                    nc.scalar.activation(att[:, i, :], s_pos[:], ACT.Copy, scale=ab[:, h, 1, i:i + 1]).then_inc(att_low.sem, 1)
                for i in range(KD):
                    act.wait_ge(att_val.sem, att_val.after(pair, ("ATT", layer, h), i + 1))
                    nc.scalar.activation(att_h[:, i, :], att[:, i, :], ACT.Copy).then_inc(att_hi.sem, 1)

            def rd(pair, layer, h):
                act.wait_ge(yb[1].full, yb[1].filled(pair, ("RD", layer, h)))
                keys = [k for k in ORDERS["DVE"] if k[0] == "RES"]
                n = keys.index(("RES", layer, h))
                if n > 0:
                    act.wait_ge(ub[1].free, ub[1].read(pair, ("U",) + keys[n - 1][1:]))
                elif not first(pair):
                    act.wait_ge(ub[1].free, ub[1].read(pair - 1, ("U",) + keys[-1][1:]))
                nc.scalar.activation(inv_den_bc[:], yb[1].t[:], ACT.Copy).then_inc(yb[1].free, 1)

            def res(pair, layer, h):
                for ot in range(NT):
                    act.wait_ge(ub[ot].free, ub[ot].read(pair, ("U", layer, h)))
                    nc.scalar.activation(u[:, ot, :], u[:, ot, :], ACT.Relu, bias=bm[:, layer, ot:ot + 1]).then_inc(relued.sem, 1)
                rstd_of(1, act_b, pair, ("RES", layer, h), h)

            def nrm(pair, layer, h):
                x_split(1, pair, ("NRM", layer, h), h, x2)

            def l3(pair, h):
                rstd_of(1, act_b, pair, ("L3", h), h)

            schedule(act, "ACT", {"XT": xt_split, "ZL": project("ZL", z_h), "ZG": project("ZG", z_h), "V": project("V", v_h),
                           "GL": gl, "HB": hb, "KT": kt, "KV": kv, "KVN": kvn, "Y": y, "QK": qk_rows,
                           "ATT": att_split, "RD": rd, "RES": res, "NRM": nrm, "L3": l3}, ((act_f,), (act_b,)))

        @block.vector
        def _(dve):
            sub, mult, add, vmax, vmin = ALU.subtract, ALU.mult, ALU.add, ALU.max, ALU.min
            nc.vector.memset(eps_col[:], LN_EPS)
            dve.wait_ge(small_in, 16 * 8)
            nc.vector.memset(ones[:], 1.0).then_inc(setup_dve, 1)
            dve.wait_ge(w_in2, 16)
            dve.wait_ge(setup_act, 4)
            nc.vector.tensor_tensor(wl_l[:], att[:], f32(wl_h[:]), sub).then_inc(setup_dve, 1)
            nc.vector.tensor_scalar(tiny[:, 3:4], tiny[:, 2:3], 1.0, None, add).then_inc(setup_dve, 1)
            nc.vector.tensor_tensor(grav[:, 0, :, :], offdiag[:], offdiag[:], mult).then_inc(setup_dve, 1)
            nc.vector.tensor_tensor(aq_l[:], x_small_view(xt_in, NT, AQ), f32(aq_h[:]), sub).then_inc(setup_dve, 1)
            dve.wait_ge(setup_dve, 4)
            nc.vector.reciprocal(w_lang_col[:], tiny[:, 3:4]).then_inc(setup_dve, 1)
            for j in range(NT):
                d = offdiag[:, j, j * P:(j + 1) * P]
                own = lang[:, 0, j, 0:P]
                nc.vector.tensor_scalar(own, ident[:], -1.0, 1.0, mult, add).then_inc(setup_own, 1)
                dve.wait_ge(setup_own, 2 * j + 1)
                nc.vector.tensor_tensor(d, d, own, mult).then_inc(setup_own, 1)
            dve.wait_ge(setup_dve, 6)
            nc.vector.tensor_scalar(w_grav_col[:], w_lang_col[:], -1.0, 1.0, mult, add).then_inc(setup_own, 1)
            dve.wait_ge(setup_own, 5)
            for k in range(KD):
                dve.wait_ge(setup_act, 5 + k)
                mm = nc.vector.tensor_tensor(wv_l[:, k, :], [pb, gb][k // 2][k % 2].t[:], f32(wv_h[:, k, :]), sub)
            mm.then_inc(setup_dve, 1)
            dve.wait_ge(setup_act, 9)
            nc.vector.tensor_tensor(wg_l[:], att[:], f32(wg_h[:]), sub).then_inc(setup_dve, 1)
            dve.wait_ge(setup_act, 10)
            nc.vector.tensor_tensor(a2_l[:], grav[:, 0, :, :], f32(a2_h[:]), sub).then_inc(setup_dve, 1)
            dve.wait_ge(setup_dve, 9)

            def project(kind, dst_h, dst_l):
                def do(pair, e):
                    b = pb[e % 2]
                    dve.wait_ge(proj_hi.sem, proj_hi.after(pair, (kind, e)))
                    nc.vector.tensor_tensor(dst_l[:, e, :], b.t[:], f32(dst_h[:, e, :]), sub).then_inc(b.free, 1)
                return do

            def diagonal(b, h, to, scratch):
                for j in range(NT):
                    ins = nc.vector.scalar_tensor_tensor(scratch[:, h, j, 0:P], b.t[:, j * N + j * P:j * N + (j + 1) * P], 1.0,
                                                         ident[:], mult, mult, accum_out=cols[:, h, to, j:j + 1])
                dve_f.link(dve, ins)

            def gl(pair, h):
                b = gb[h]
                dve.wait_ge(b.full, b.filled(pair, ("GL", h)))
                if not first(pair):
                    dve.wait_ge(pb[h].full, pb[h].filled(pair - 1, ("KT", h)))
                diagonal(b, h, SS, lang)
                nc.vector.tensor_scalar(cols[:, h, SS, :], cols[:, h, SS, :], EPS * EPS, None, vmax).then_inc(lang_sq.sem, 1)
                nc.vector.scalar_tensor_tensor(lang[:, h, :, :], b.t[:].rearrange("p (t n) -> p t n", t=NT), 0.0, offdiag[:],
                                               vmax, mult).then_inc(b.free, 1)
                dve.wait_ge(b.free, b.read(pair, ("GL", h)))

            def row_factor(h, deg, to, weight):
                dve_f.link(dve, nc.vector.tensor_scalar(cols[:, h, deg, :], cols[:, h, deg, :], EPS, None, vmax))
                dve_f.link(dve, nc.vector.reciprocal(cols[:, h, to, :], cols[:, h, deg, :]))
                dve_f.link(dve, nc.vector.tensor_scalar(cols[:, h, to, :], cols[:, h, to, :], weight[:, 0:1], None, mult))

            def rb(pair, h):
                b = pb[h]
                dve.wait_ge(b.full, b.filled(pair, ("RB", h)))
                for j in range(NT):
                    ins = nc.vector.scalar_tensor_tensor(lang[:, h, j, :], lang[:, h, j, :], cols[:, h, R, j:j + 1], b.t[:, 0:N],
                                                         mult, mult, accum_out=cols[:, h, DEGL, j:j + 1])
                ins.then_inc(b.free, 1)
                dve.wait_ge(b.free, b.read(pair, ("RB", h)))
                row_factor(h, DEGL, CL, w_lang_col)

            def gg(pair, h):
                b = gb[h]
                dve.wait_ge(b.full, b.filled(pair, ("GG", h)))
                diagonal(b, h, SQ, grav)
                nc.vector.tensor_scalar(cols[:, h, HSQ, :], cols[:, h, SQ, :], 0.5, None, mult).then_inc(grav_hsq.sem, 1)

            def hb(pair, h):
                b = gb[h]
                dve.wait_ge(pb[h].free, pb[h].read(pair, ("HB", h)))
                dve.wait_ge(grav_hsq.sem, grav_hsq.after(pair, ("GG", h)))
                for j in range(NT):
                    ins = nc.vector.scalar_tensor_tensor(grav[:, h, j, :], b.t[:, j * N:(j + 1) * N], cols[:, h, HSQ, j:j + 1],
                                                         half_sq_bc[:, h, :], sub, sub)
                ins.then_inc(b.free, 1)
                dve.wait_ge(b.free, b.read(pair, ("GG", h)))
                nc.vector.tensor_scalar(grav[:, h, :, :], grav[:, h, :, :], 0.0, None, vmin).then_inc(grav_d.sem, 1)

            def eg(pair, h):
                dve.wait_ge(grav_e.sem, grav_e.after(pair, ("HB", h)))
                for j in range(NT):
                    ins = nc.vector.scalar_tensor_tensor(grav[:, h, j, :], grav[:, h, j, :], 1.0, offdiag[:, j, :], mult, mult,
                                                         accum_out=cols[:, h, DEGG, j:j + 1])
                dve_f.link(dve, ins)
                row_factor(h, DEGG, CG, w_grav_col)
                for j in range(NT):
                    ins = nc.vector.tensor_scalar(grav[:, h, j, :], grav[:, h, j, :], cols[:, h, CG, j:j + 1], None, mult)
                dve_f.link(dve, ins)
                for j in range(NT):
                    ins = nc.vector.scalar_tensor_tensor(lang[:, h, j, :], lang[:, h, j, :], cols[:, h, CL, j:j + 1],
                                                         grav[:, h, j, :], mult, add)
                ins.then_inc(graph.sem, 1)

            def kt(pair, h):
                dve.wait_ge(kt_hi.sem, kt_hi.after(pair, ("KT", h)))
                nc.vector.tensor_tensor(kt_l[:, h, :, :], pb[h].t[:].rearrange("p (t n) -> p t n", t=NT), f32(kt_h[:, h, :, :]),
                                        sub).then_inc(pb[h].free, 1)

            def low(s, pair, key, h, src):
                dve.wait_ge(x_hi[s].sem, x_hi[s].after(pair, key, 2))
                t = NT * h + 1
                nc.vector.tensor_tensor(x_l[:, t, :], src[:, t, :], f32(x_h[:, t, :]), sub).then_inc(x_lo[s][1].sem, 1)

            def normalise(s, pair, stat_key, key, h, x):
                dve.wait_ge(rstd_known[s].sem, rstd_known[s].after(pair, stat_key))
                for j in range(NT):
                    t = x[:, NT * h + j, :]
                    nc.vector.tensor_scalar(t, t, mean_var[:, s, h, j, 0:1], rstd[:, s, h, j:j + 1], sub,
                                            mult).then_inc(normed[s].sem, 1)

            def kv(pair, h):
                dve.wait_ge(x0_loaded[h], 16 * pair + 16)
                for j in range(NT):
                    b = (gb, pb)[h][j]
                    t = x1[:, NT * h + j, :]
                    dve.wait_ge(b.full, b.filled(pair, ("KV", h)))
                    nc.vector.tensor_tensor(t, b.t[:], t, add).then_inc(b.free, 1)
                    dve.wait_ge(b.free, b.read(pair, ("KV", h)))
                for j in range(NT):
                    ins = nc.vector.bn_stats(stats[:, 0, h, j, :], x1[:, NT * h + j, :])
                dve_f.link(dve, ins)
                dve_carrier()
                for j in range(NT):
                    ins = nc.vector.bn_aggr(mean_var[:, 0, h, j, :], stats[:, 0, h, j, :])
                ins.then_inc(var_known[0].sem, 1)

            def kvn(pair, h):
                normalise(0, pair, ("KV", h), ("KVN", h), h, x1)
                low(0, pair, ("KVN", h), h, x1)

            def y(pair, layer, h):
                for i in range(KD):
                    b = yb[i % 2]
                    dve.wait_ge(y_hi.sem, y_hi.after(pair, ("Y", layer, h), i + 1))
                    nc.vector.tensor_tensor(y_l[:, h, i, :], b.t[:, 0:YW], f32(y_h[:, h, i, :]), sub).then_inc(b.free, 1)
                for n in range(2):
                    dve.wait_ge(yb[n].free, yb[n].read(pair, ("Y", layer, h, n + 2)))
                c = q_cols(layer)
                nc.vector.tensor_tensor(qk[:, h, :, :], f32(y_h[:, h, :, c]), f32(y_l[:, h, :, c]), add).then_inc(qk_cols.sem, 1)

            def qk_rows(pair, layer, h):
                b = yb[0]
                dve.wait_ge(b.full, b.filled(pair, ("QK", layer, h)))
                nc.vector.reduce_max(qs[:, h, 0:1], b.t[:], AX_X).then_inc(b.free, 1)
                dve.wait_ge(b.free, b.read(pair, ("QK", layer, h)))
                nc.vector.tensor_scalar(qs[:, h, 1:2], qs[:, h, 0:1], -1.0, None, mult)
                nc.vector.tensor_scalar(qs[:, h, 2:2 + KD], qk[:, h, :, 0], qs[:, h, 0:1], None, sub).then_inc(q_max.sem, 1)

            def attention(pair, layer, h):
                key = ("ATT", layer, h)
                dve.wait_ge(factors.sem, factors.after(pair, ("QK", layer, h)))

                def value(i):
                    dve.wait_ge(att_low.sem, att_low.after(pair, key, i + 1))
                    nc.vector.scalar_tensor_tensor(att[:, i, :], s_neg[:], ab[:, h, 0, i:i + 1], att[:, i, :], mult,
                                                   vmax).then_inc(att_val.sem, 1)

                def low(i):
                    dve.wait_ge(att_hi.sem, att_hi.after(pair, key, i + 1))
                    nc.vector.tensor_tensor(att_l[:, i, :], att[:, i, :], f32(att_h[:, i, :]), sub).then_inc(att_lo.sem, 1)

                value(0)
                value(1)
                low(0)
                value(2)
                low(1)
                value(3)
                low(2)
                low(3)

            def den(pair, layer, h):
                b = yb[0]
                dve.wait_ge(b.full, b.filled(pair, ("DEN", layer, h)))
                nc.vector.reciprocal(inv_den[:], b.t[:, 0:KD]).then_inc(b.free, 1)

            def res(pair, layer, h):
                dve.wait_ge(yb[1].free, yb[1].read(pair, ("RD", layer, h)))
                for ot in range(NT):
                    b = ub[ot]
                    dve.wait_ge(b.full, b.filled(pair, ("U", layer, h)))
                    nc.vector.tensor_tensor(u[:, ot, :], b.t[:], inv_den_bc[:], mult).then_inc(b.free, 1)
                if layer == 0 and not first(pair):
                    dve.wait_ge(stored[h], 16 * pair)
                src = x1 if layer == 0 else x2
                dve.wait_ge(relued.sem, relued.after(pair, ("RES", layer, h), 2))
                nc.vector.tensor_tensor(x2[:, NT * h + 1, :], u[:, 1, :], src[:, NT * h + 1, :], add).then_inc(added[1].sem, 1)
                for j in (1, 0):
                    dve.wait_ge(added[j].sem, added[j].after(pair, ("RES", layer, h)))
                    ins = nc.vector.bn_stats(stats[:, 1, h, j, :], x2[:, NT * h + j, :])
                dve_b.link(dve, ins)
                dve_carrier()
                for j in range(NT):
                    ins = nc.vector.bn_aggr(mean_var[:, 1, h, j, :], stats[:, 1, h, j, :])
                ins.then_inc(var_known[1].sem, 1)

            def nrm(pair, layer, h):
                normalise(1, pair, ("RES", layer, h), ("NRM", layer, h), h, x2)
                low(1, pair, ("NRM", layer, h), h, x2)

            def l3(pair, h):
                for mt in range(NT):
                    b = ub[mt]
                    t = x2[:, NT * h + mt, :]
                    dve.wait_ge(b.full, b.filled(pair, ("L3", h)))
                    dve.wait_ge(biased.sem, biased.after(pair, ("NRM", 1, h), mt + 1))
                    nc.vector.tensor_tensor(t, b.t[:], t, add).then_inc(b.free, 1)
                    dve.wait_ge(b.free, b.read(pair, ("L3", h)))
                    ins = nc.vector.bn_stats(stats[:, 1, h, mt, :], t)
                dve_b.link(dve, ins)
                dve_carrier()
                for j in range(NT):
                    ins = nc.vector.bn_aggr(mean_var[:, 1, h, j, :], stats[:, 1, h, j, :])
                ins.then_inc(var_known[1].sem, 1)

            def l3n(pair, h):
                normalise(1, pair, ("L3", h), ("L3N", h), h, x2)

            schedule(dve, "DVE", {"ZL": project("ZL", z_h, z_l), "ZG": project("ZG", z_h, z_l),
                           "V": project("V", v_h, v_l), "GL": gl, "RB": rb, "GG": gg, "HB": hb, "EG": eg, "KT": kt,
                           "KV": kv, "KVN": kvn, "Y": y, "QK": qk_rows, "ATT": attention, "DEN": den, "RES": res,
                           "NRM": nrm, "L3": l3, "L3N": l3n}, ((dve_f,), (dve_b,)))

        @block.gpsimd
        def _(pool):
            def attention(pair, layer, h):
                key = ("ATT", layer, h)
                keys = [k for k in ORDERS["DVE"] if k[0] == "ATT"]
                n = keys.index(key)
                if n > 0:
                    pool.wait_ge(yb[0].full, yb[0].filled(pair, ("DEN",) + keys[n - 1][1:]))
                elif not first(pair):
                    pool.wait_ge(yb[0].full, yb[0].filled(pair - 1, ("DEN",) + keys[-1][1:]))
                pool.wait_ge(att_val.sem, att_val.after(pair, key, 2))
                pool_b.link(pool, nc.gpsimd.tensor_tensor(den_sum[:], att[:, 0, :], att[:, 1, :], ALU.add))
                pool.wait_ge(att_val.sem, att_val.after(pair, key, 3))
                pool_b.link(pool, nc.gpsimd.tensor_tensor(den_sum[:], den_sum[:], att[:, 2, :], ALU.add))
                pool.wait_ge(att_val.sem, att_val.after(pair, key, 4))
                nc.gpsimd.tensor_tensor(den_sum[:], den_sum[:], att[:, 3, :], ALU.add).then_inc(summed.sem, 1)

            def xt_split(pair, c):
                pool.wait_ge(xt_hi.sem, xt_hi.after(pair, ("XT", c)))
                k = slice(2 * c, 2 * c + 2)
                nc.gpsimd.tensor_tensor(xt_l[:, k, :], xt_in[:], f32(xt_h[:, k, :]), ALU.subtract).then_inc(xt_lo.sem, 1)

            def low(s, pair, key, h, src):
                pool.wait_ge(x_hi[s].sem, x_hi[s].after(pair, key, 1))
                t = NT * h
                nc.gpsimd.tensor_tensor(x_l[:, t, :], src[:, t, :], f32(x_h[:, t, :]), ALU.subtract).then_inc(x_lo[s][0].sem, 1)

            def res(pair, layer, h):
                if layer == 0 and not first(pair):
                    pool.wait_ge(stored[h], 16 * pair)
                src = x1 if layer == 0 else x2
                pool.wait_ge(relued.sem, relued.after(pair, ("RES", layer, h), 1))
                nc.gpsimd.tensor_tensor(x2[:, NT * h, :], u[:, 0, :], src[:, NT * h, :], ALU.add).then_inc(added[0].sem, 1)

            def kvn(pair, h):
                low(0, pair, ("KVN", h), h, x1)

            def nrm(pair, layer, h):
                low(1, pair, ("NRM", layer, h), h, x2)
                if layer == 1:
                    for j in range(NT):
                        pool.wait_ge(x_lo[1][j].sem, x_lo[1][j].after(pair, ("NRM", 1, h)))
                        t = x2[:, NT * h + j, :]
                        nc.gpsimd.tensor_tensor(t, t, bias_bc[:], ALU.add).then_inc(biased.sem, 1)

            schedule(pool, "POOL", {"XT": xt_split, "ATT": attention, "RES": res, "KVN": kvn, "NRM": nrm}, ((), (pool_b,)))


def x_small_view(t, a, b):
    return t[:].rearrange("p c n -> p (c n)")[:, 0:a * b].rearrange("p (a b) -> p a b", a=a)


def kernel(x, adj, L0_gnn_W_lang, L0_gnn_W_grav, L0_gnn_W_V, L0_gnn_W_O, L0_gnn_gate_logit, L0_gnn_log_sigma,
           L1_gnn_wq, L1_gnn_wk, L1_gnn_bm, L2_gnn_wq, L2_gnn_wk, L2_gnn_bm, L3_gnn_bias):
    import numpy as np
    import concourse.bacc as bacc
    from concourse.bass_utils import run_bass_kernel_spmd

    a = {k: np.asarray(v) for k, v in locals().items() if k not in ("np", "bacc", "run_bass_kernel_spmd")}
    B, N, D = a["x"].shape
    PAIRS, NT, KD = B // 2, N // P, D // P
    col = lambda v: np.ascontiguousarray(v.reshape(-1, P).T)
    adj_t = a["adj"].T
    arrays = {
        "xn": np.ascontiguousarray(a["x"].reshape(PAIRS, 2 * NT, P, D).transpose(0, 2, 1, 3)),
        "xt": np.ascontiguousarray(a["x"].reshape(PAIRS, 2 * N, KD, P).transpose(0, 3, 2, 1)),
        "adj": np.ascontiguousarray(a["adj"]),
        "adjq": np.ascontiguousarray(np.concatenate(
            [a["L1_gnn_wq"][:, None], a["L1_gnn_wk"][:, None], adj_t, a["L2_gnn_wq"][:, None], a["L2_gnn_wk"][:, None]], axis=1)),
        "w_l": np.ascontiguousarray(a["L0_gnn_W_lang"].T),
        "w_g": np.ascontiguousarray(a["L0_gnn_W_grav"].T),
        "w_v": np.ascontiguousarray(a["L0_gnn_W_V"]),
        "w_o": np.ascontiguousarray(a["L0_gnn_W_O"].T),
        "gate": np.ascontiguousarray(np.broadcast_to(a["L0_gnn_gate_logit"].reshape(1, 1), (P, 1))),
        "sigma": np.ascontiguousarray(np.broadcast_to(a["L0_gnn_log_sigma"].reshape(1, 1), (P, 1))),
        "bm1": col(a["L1_gnn_bm"]),
        "bm2": col(a["L2_gnn_bm"]),
        "bias3": np.ascontiguousarray(np.broadcast_to(a["L3_gnn_bias"][None, :], (P, D))),
        "ident": np.eye(P, dtype=np.float32),
    }
    nc = bacc.Bacc("TRN2", target_bir_lowering=False, num_devices=1, dynamic_dma_scratch_size=1024)
    args = [nc.dram_tensor(f"in_{k}", v.shape, mybir.dt.from_np(v.dtype), kind="ExternalInput").ap() for k, v in arrays.items()]
    args.append(nc.dram_tensor("out", (PAIRS, P, 2 * NT, D), F32, kind="ExternalOutput").ap())
    resnorm_kernel(nc, *args)
    r = run_bass_kernel_spmd(nc, [{f"in_{k}": v for k, v in arrays.items()}], core_ids=[0])
    got = r.results[0]["out"]
    return np.ascontiguousarray(got.transpose(0, 2, 1, 3)).reshape(B, N, D)
```

```python
from contextlib import ExitStack

import concourse.bass as bass
from concourse import mybir

F32 = mybir.dt.float32
F32R = mybir.dt.float32r
ALU = mybir.AluOpType
ACT = mybir.ActivationFunctionType
AX_X = mybir.AxisListType.X

P = 128
LEAK = 0.01
LN_EPS = 1e-5
EPS = 1e-8

ORDERS = {
    "PE": """
    V.0 YA.0.0 GL.0 YB.0.0 V.1 QK.0.0 RB.0 GL.1 YA.0.1 YB.0.1 ZG.0 RB.1 QK.0.1 U.0.0.0 U.0.0.1 DEN.0.0 ZG.1
    ZG.2 U.0.1.0 U.0.1.1 DEN.0.1 ZG.3 YA.1.0 YB.1.0 V.2 QK.1.0 GG.0 YA.1.1 HB.0 YB.1.1 GG.1 QK.1.1 U.1.0.0 V.3
    U.1.0.1 DEN.1.0 KT.0 HB.1 KV.0 U.1.1.0 KT.1 U.1.1.1 DEN.1.1 KV.1 ZL.0 ZL.1 ZL.2 L3.0 ZL.3 L3.1
    """,
    "ACT": """
    YA.0.0 V.0 YB.0.0 GL.0 V.1 QK.0.0 YA.0.1 AT.0.0 YB.0.1 GL.1 AH.0.0.0 AH.0.0.1 ZG.0 DH.0.0 QK.0.1 AT.0.1
    AH.0.1.0 DEN.0.0 ZG.1 AH.0.1.1 RES.0.0 DH.0.1 ZG.2 STA.0.0 NRM.0.0 DEN.0.1 RES.0.1 YA.1.0 YB.1.0 ZG.3
    STA.0.1 V.2 NRM.0.1 QK.1.0 YA.1.1 AT.1.0 YB.1.1 AH.1.0.0 AH.1.0.1 HB.0 DH.1.0 QK.1.1 V.3 AT.1.1 AH.1.1.0
    KT.0 DEN.1.0 HB.1 XT.0 RES.1.0 AH.1.1.1 DH.1.1 KT.1 DEN.1.1 XT.1 STA.1.0 KV.0 ZL.0 RES.1.1 NRM.1.0 KV.1
    STA.1.1 ZL.1 ZL.2 NRM.1.1 L3.0 KVN.0 ZL.3 L3.1 KVN.1
    """,
    "DVE": """
    YA.0.0 GL.0 V.0 YB.0.0 QK.0.0 V.1 RB.0 GL.1 YA.0.1 AV.0.0.0 AV.0.0.1 YB.0.1 AL.0.0.0 QK.0.1 AL.0.0.1 RB.1
    ZG.0 AV.0.1.0 AV.0.1.1 AL.0.1.0 RES.0.0 AL.0.1.1 ZG.1 STA.0.0 NRM.0.0 ZG.2 LOW.0.0 RES.0.1 YA.1.0 STA.0.1
    YB.1.0 ZG.3 NRM.0.1 QK.1.0 LOW.0.1 V.2 GG.0 YA.1.1 AV.1.0.0 AV.1.0.1 YB.1.1 AL.1.0.0 HB.0 QK.1.1 AL.1.0.1
    EG.0 GG.1 V.3 AV.1.1.0 AV.1.1.1 AL.1.1.0 KT.0 HB.1 RES.1.0 EG.1 AL.1.1.1 STA.1.0 KT.1 KV.0 KV.1 RES.1.1
    NRM.1.0 ZL.0 STA.1.1 LOW.1.0 NRM.1.1 ZL.1 ZL.2 LOW.1.1 L3.0 KVN.0 L3.1 KVL.0 ZL.3 L3N.0 KVN.1 L3N.1 KVL.1
    """,
    "POOL": """
    DS.0.0 DL.0.0 DS.0.1 RES.0.0 DL.0.1 NRM.0.0 RES.0.1 NRM.0.1 DS.1.0 DL.1.0 DS.1.1 XT.0 RES.1.0 DL.1.1 XT.1
    RES.1.1 NRM.1.0 NRM.1.1 KVN.0 KVN.1
    """,
    "SP": """
    RES.0.0 RES.0.1 XT.0 XT.1 L3N.0 L3N.1
    """,
}
ORDERS = {e: [(t[0],) + tuple(int(x) for x in t[1:]) for t in (w.split(".") for w in text.split())]
          for e, text in ORDERS.items()}
FRONT = {"XT", "ZL", "ZG", "V", "GL", "GG", "RB", "HB", "EG", "KT", "KV", "KVN", "KVL"}
AHEAD = ("XT", "ZL")


class Count:

    def __init__(self, keys, pairs):
        self.keys, self.last = keys, pairs - 1
        self.before = [k for k in keys if stage_of(k) in AHEAD]

    def upto(self, pair, key):
        if stage_of(key) in AHEAD:
            if first(pair):
                return self.before.index(key) + 1
            return len(self.before) + (pair - 1) * len(self.keys) + self.keys.index(key) + 1
        keys = self.keys
        if isinstance(pair, int) and pair == self.last:
            keys = [k for k in keys if stage_of(k) not in AHEAD]
        return len(self.before) + pair * len(self.keys) + keys.index(key) + 1


class Signal:

    def __init__(self, sem, engine, pairs, stages, each=1, step=1):
        self.sem, self.each, self.step = sem, each, step
        self.count = Count([k for k in ORDERS[engine] if k[0] in stages or k[:2] in stages], pairs)

    def after(self, pair, key, k=None):
        short = 0 if k is None else self.each - k
        return (self.count.upto(pair, key) * self.each - short) * self.step


class Bank:

    def __init__(self, tensor, full, free, uses, pairs):
        self.t, self.full, self.free = tensor, full, free
        self.count = Count(uses, pairs)

    def filled(self, pair, key):
        return self.count.upto(pair, key)

    read = filled


def stage_of(key):
    return key[0]


def first(pair):
    return isinstance(pair, int) and pair == 0


class Chain:

    def __init__(self, sem):
        self.sem, self.k, self.n, self.pair = sem, 0, None, 0

    def begin(self, pair):
        if self.n is None and not (isinstance(pair, int) and pair == 0):
            self.n = self.k
        self.pair, self.k = pair, 0

    def link(self, eng, ins):
        ins.then_inc(self.sem, 1)
        self.k += 1
        base = 0 if self.n is None else self.pair * self.n
        eng.wait_ge(self.sem, base + self.k)


def uses_of(bank):
    kind, n = bank
    out = []
    for key in ORDERS["PE"]:
        s, a = key[0], key[1:]
        if kind == "P":
            if s in ("ZL", "ZG", "V") and a[0] % 2 == n:
                out.append(key)
            if s in ("RB", "HB", "KT") and a[0] == n:
                out.append(key)
            if s == "KV" and a[0] == 1:
                out.append(key)
        if kind == "G":
            if s in ("GL", "GG") and a[0] == n:
                out.append(key)
            if s == "KV" and a[0] == 0:
                out.append(key)
        if kind == "Y":
            if s in ("YA", "YB", "QK") or (s == "DEN" and n == 0):
                out.append(key)
        if kind == "U" and (s == "L3" or (s == "U" and a[2] == 1)):
            out.append(key)
    return out


def resnorm_kernel(nc, xn, xt, adj, adjq, w_l, w_g, w_v, w_o, gate, sigma, bm1, bm2, bias3, ident_in, out):
    PAIRS = xn.shape[0]
    D = xn.shape[3]
    KD = D // P
    N = adj.shape[0]
    NT = N // P
    AQ = adjq.shape[1]
    YW = N + 2

    with ExitStack() as ctx:
        def sb(name, shape, dt=F32):
            return ctx.enter_context(nc.sbuf_tensor(name, shape, dt))

        def sem(name):
            return ctx.enter_context(nc.semaphore(name))

        wl_h, wl_l = sb("wl_h", [P, KD, D], F32R), sb("wl_l", [P, KD, D], F32R)
        wg_h, wg_l = sb("wg_h", [P, KD, D], F32R), sb("wg_l", [P, KD, D], F32R)
        wv_h, wv_l = sb("wv_h", [P, KD, D], F32R), sb("wv_l", [P, KD, D], F32R)
        aq_h, aq_l = sb("aq_h", [P, NT, AQ], F32R), sb("aq_l", [P, NT, AQ], F32R)
        a2_h, a2_l = sb("a2_h", [P, NT, N], F32R), sb("a2_l", [P, NT, N], F32R)
        offdiag = sb("offdiag", [P, NT, N])
        ident = sb("ident", [P, P])
        ones = sb("ones", [P, P], F32R)
        bias_bc = sb("bias_bc", [P, D])
        bm = sb("bm", [P, 2, NT])
        w_lang_col, w_grav_col = sb("w_lang_col", [P, 1]), sb("w_grav_col", [P, 1])
        inv_s2, neg_inv_s2 = sb("inv_s2", [P, 1]), sb("neg_inv_s2", [P, 1])
        eps_col = sb("eps_col", [P, 1])
        tiny = sb("tiny", [P, 4])
        carrier = sb("carrier", [P, 1])

        xt_in = sb("xt_in", [P, 2, D])
        xt_h, xt_l = sb("xt_h", [P, KD, D], F32R), sb("xt_l", [P, KD, D], F32R)
        z_h, z_l = sb("z_h", [P, KD, D], F32R), sb("z_l", [P, KD, D], F32R)
        v_h, v_l = sb("v_h", [P, KD, D], F32R), sb("v_l", [P, KD, D], F32R)
        lang = sb("lang", [P, 2, NT, N])
        grav = sb("grav", [P, 2, NT, N])
        half_sq_bc = sb("half_sq_bc", [P, 2, N])
        kt_h, kt_l = sb("kt_h", [P, 2, NT, N], F32R), sb("kt_l", [P, 2, NT, N], F32R)
        cols = sb("cols", [P, 2, 12, NT])
        SS, LNS, R, SQ, HSQ, DEGL, CL, DEGG, CG = range(9)

        x1 = sb("x1", [P, 2 * NT, D])
        x2 = sb("x2", [P, 2 * NT, D])
        x_h, x_l = sb("x_h", [P, 2 * NT, D], F32R), sb("x_l", [P, 2 * NT, D], F32R)
        stats = sb("stats", [P, 2, 2, NT, 6])
        mean_var = sb("mean_var", [P, 2, 2, NT, 2])
        log_var = sb("log_var", [P, 2, 2, NT])
        rstd = sb("rstd", [P, 2, 2, NT])

        y_h, y_l = sb("y_h", [P, 2, KD, YW], F32R), sb("y_l", [P, 2, KD, YW], F32R)
        qk = sb("qk", [P, 2, KD, 2])
        qs = sb("qs", [P, 2, 2 + KD])
        ab = sb("ab", [P, 2, 2, KD])
        s_neg, s_pos = sb("s_neg", [P, D]), sb("s_pos", [P, D])
        att = sb("att", [P, KD, D])
        att_h, att_l = sb("att_h", [P, KD, D], F32R), sb("att_l", [P, KD, D], F32R)
        den_sum = sb("den_sum", [P, D])
        den_h, den_l = sb("den_h", [P, D], F32R), sb("den_l", [P, D], F32R)
        inv_den_bc = sb("inv_den_bc", [P, D])
        u = sb("u", [P, NT, D])

        def bank(kind, n):
            name = f"{kind}{n}".lower()
            t = ctx.enter_context(nc.psum_tensor("bank_" + name, [P, D], F32))
            return Bank(t, sem(name + "_full"), sem(name + "_free"), uses_of((kind, n)), PAIRS)

        pb = [bank("P", 0), bank("P", 1)]
        gb = [bank("G", 0), bank("G", 1)]
        yb = [bank("Y", 0), bank("Y", 1)]
        ub = [bank("U", 0), bank("U", 1)]

        w_in, setup_wov, setup_act, setup_dve = sem("w_in"), sem("setup_wov"), sem("setup_act"), sem("setup_dve")
        wl_in, wg_in = sem("wl_in"), sem("wg_in")
        small_in, setup_own = sem("small_in"), sem("setup_own")
        xt_loaded = Signal(sem("xt_loaded"), "SP", PAIRS, ("XT",), step=16)
        x0_loaded = [sem("x0_loaded_0"), sem("x0_loaded_1")]
        stored = [sem("stored_0"), sem("stored_1")]
        xt_hi = Signal(sem("xt_hi"), "ACT", PAIRS, ("XT",))
        xt_lo = Signal(sem("xt_lo"), "POOL", PAIRS, ("XT",))
        proj_hi = Signal(sem("proj_hi"), "ACT", PAIRS, ("ZL", "ZG", "V"))
        lang_sq = Signal(sem("lang_sq"), "DVE", PAIRS, ("GL",))
        lang_r = Signal(sem("lang_r"), "ACT", PAIRS, ("GL",))
        grav_hsq = Signal(sem("grav_hsq"), "DVE", PAIRS, ("GG",))
        grav_e = Signal(sem("grav_e"), "ACT", PAIRS, ("HB",))
        graph = Signal(sem("graph"), "DVE", PAIRS, ("EG",))
        kt_hi = Signal(sem("kt_hi"), "ACT", PAIRS, ("KT",))
        added = [Signal(sem("added_0"), "POOL", PAIRS, ("RES",)), Signal(sem("added_1"), "DVE", PAIRS, ("STA",))]
        var_known = [Signal(sem("f_var"), "DVE", PAIRS, ("KV",)), Signal(sem("b_var"), "DVE", PAIRS, ("STA", "L3"))]
        rstd_known = [Signal(sem("f_rstd"), "ACT", PAIRS, ("KV",)), Signal(sem("b_rstd"), "ACT", PAIRS, ("STA", "L3"))]
        normed = [Signal(sem("f_normed"), "DVE", PAIRS, ("KVN",), 2), Signal(sem("b_normed"), "DVE", PAIRS, ("NRM", "L3N"), 2)]
        x_hi = [Signal(sem("f_x_hi"), "ACT", PAIRS, ("KVN",), 2), Signal(sem("b_x_hi"), "ACT", PAIRS, ("NRM",), 2)]
        x_lo = [[Signal(sem("f_x_lo_0"), "POOL", PAIRS, ("KVN",)), Signal(sem("f_x_lo_1"), "DVE", PAIRS, ("KVL",))],
                [Signal(sem("b_x_lo_0"), "POOL", PAIRS, ("NRM",)), Signal(sem("b_x_lo_1"), "DVE", PAIRS, ("LOW",))]]
        biased = Signal(sem("biased"), "POOL", PAIRS, (("NRM", 1),), 2)
        y_hi = Signal(sem("y_hi"), "ACT", PAIRS, ("YA", "YB"), 2)
        qk_cols = Signal(sem("qk_cols"), "DVE", PAIRS, ("YB",))
        q_max = Signal(sem("q_max"), "DVE", PAIRS, ("QK",))
        factors = Signal(sem("factors"), "ACT", PAIRS, ("QK",))
        att_low = Signal(sem("att_low"), "ACT", PAIRS, ("AT",), 4)
        att_val = Signal(sem("att_val"), "DVE", PAIRS, ("AV",), 2)
        att_hi = Signal(sem("att_hi"), "ACT", PAIRS, ("AH",), 2)
        att_lo = Signal(sem("att_lo"), "DVE", PAIRS, ("AL",), 2)
        summed = Signal(sem("summed"), "POOL", PAIRS, ("DS",))
        den_hi = Signal(sem("den_hi"), "ACT", PAIRS, ("DH",))
        den_lo = Signal(sem("den_lo"), "POOL", PAIRS, ("DL",))
        inverted = Signal(sem("inverted"), "ACT", PAIRS, ("DEN",))
        relued = Signal(sem("relued"), "ACT", PAIRS, ("RES",), 2)
        dve_f, dve_b = Chain(sem("dve_f")), Chain(sem("dve_b"))
        act_f, act_b = Chain(sem("act_f")), Chain(sem("act_b"))
        pool_b = Chain(sem("pool_b"))

        def f32(ap):
            return ap.bitcast(F32)

        def y_cols(layer, ot):
            at = (2 if layer == 0 else 0) + ot * P
            return slice(at, at + P)

        def q_cols(layer):
            return slice(0, 2) if layer == 0 else slice(N, N + 2)

        def half_of(stage, which):
            return lambda pair, layer, h: stage(pair, layer, h, which)

        def before(pair, layer, h):
            keys = [k[1:] for k in ORDERS["PE"] if k[0] == "QK"]
            n = keys.index((layer, h))
            if n > 0:
                return (pair,) + keys[n - 1]
            return None if first(pair) else (pair - 1,) + keys[-1]

        def schedule(eng, order, stages, chains, setup=None):
            fchains, bchains = chains

            def one(front, back, ahead=True):
                for c in fchains:
                    if front is not None:
                        c.begin(front)
                for c in bchains:
                    if back is not None:
                        c.begin(back)
                for key in ORDERS[order]:
                    do = stages[key[0]]
                    if key[0] in AHEAD:
                        if front is not None and ahead:
                            do(front + 1, *key[1:])
                    elif key[0] in FRONT:
                        if front is not None:
                            do(front, *key[1:])
                    elif back is not None:
                        do(back, *key[1:])

            for key in ORDERS[order]:
                if key[0] in AHEAD:
                    stages[key[0]](0, *key[1:])
            if setup:
                setup()
            one(0, None)
            one(1, 0)
            with eng.Fori(2, PAIRS - 1) as i:
                one(i, i - 1)
            one(PAIRS - 1, PAIRS - 2, ahead=False)
            one(None, PAIRS - 1)

        def dve_carrier():
            nc.vector.memset(carrier[:, 0:1], 0.0)

        block = ctx.enter_context(nc.Block())

        @block.sync
        def _(sp):
            def load_xt(pair, c):
                if c == 1:
                    sp.wait_ge(xt_lo.sem, xt_lo.after(pair, ("XT", 0)))
                elif not first(pair):
                    sp.wait_ge(xt_lo.sem, xt_lo.after(pair - 1, ("XT", 1)))
                sp.dma_start(xt_in[:], xt[pair, :, 2 * c:2 * c + 2, :]).then_inc(xt_loaded.sem, 16)

            def load_x0(pair, h):
                if first(pair):
                    sp.wait_ge(setup_wov, 4)
                else:
                    sp.wait_ge(added[0].sem, added[0].after(pair - 1, ("RES", 0, h)))
                    sp.wait_ge(added[1].sem, added[1].after(pair - 1, ("STA", 0, h)))
                sp.dma_start(x1[:, NT * h:NT * h + NT, :], xn[pair, :, NT * h:NT * h + NT, :]).then_inc(x0_loaded[h], 16)

            def store(pair, h):
                sp.wait_ge(normed[1].sem, normed[1].after(pair, ("L3N", h)))
                sp.dma_start(out[pair, :, NT * h:NT * h + NT, :], x2[:, NT * h:NT * h + NT, :]).then_inc(stored[h], 16)

            load_xt(0, 0)
            sp.dma_start(att[:], w_l.rearrange("(t p) m -> p t m", p=P)).then_inc(wl_in, 16)
            load_xt(0, 1)
            sp.dma_start(x1[:], w_o.rearrange("(t p) m -> p t m", p=P)).then_inc(w_in, 16)
            sp.dma_start(x2[:], w_v.rearrange("(t p) m -> p t m", p=P)).then_inc(w_in, 16)
            for t, src in ((ident[:], ident_in), (offdiag[:], adj.rearrange("(t p) m -> p t m", p=P)),
                           (bias_bc[:], bias3), (bm[:, 0, :], bm1), (bm[:, 1, :], bm2),
                           (tiny[:, 0:1], gate), (tiny[:, 1:2], sigma),
                           (small_view(u, NT, AQ), adjq.rearrange("(t p) m -> p t m", p=P))):
                sp.dma_start(t, src).then_inc(small_in, 16)
            sp.wait_ge(setup_dve, 1)
            sp.dma_start(att[:], w_g.rearrange("(t p) m -> p t m", p=P)).then_inc(wg_in, 16)
            load_xt(1, 0)
            load_x0(0, 0)
            load_x0(0, 1)
            load_xt(1, 1)

            def one(front, back, ahead):
                for key in ORDERS["SP"]:
                    if key[0] == "RES" and front is not None:
                        load_x0(front, key[2])
                    if key[0] == "XT" and ahead:
                        load_xt(front + 1, key[1])
                    if key[0] == "L3N" and back is not None:
                        store(back, key[1])

            one(1, 0, True)
            with sp.Fori(2, PAIRS - 1) as i:
                one(i, i - 1, True)
            one(PAIRS - 1, PAIRS - 2, False)
            one(None, PAIRS - 1, False)
            for h in range(2):
                sp.wait_ge(stored[h], 16 * PAIRS)

        @block.tensor
        def _(pe):
            def split_product(outap, pairs, start, stop):
                last = None
                n = 3 * len(pairs)
                m = 0
                for sh, sl, mh, ml in pairs:
                    for a, b in ((sh, mh), (sh, ml), (sl, mh)):
                        last = pe.matmul(outap, a, b, start=start and m == 0, stop=stop and m == n - 1)
                        m += 1
                return last

            def take(b, pair, key):
                before = b.filled(pair, key) - 1
                if not (isinstance(before, int) and before == 0):
                    pe.wait_ge(b.free, before)

            def setup():
                pe.wait_ge(w_in, 32)
                for k in range(KD):
                    for e in range(KD):
                        mm = pe.matmul((gb + ub)[k].t[:], x2[:, e, k * P:(k + 1) * P], x1[:, e, :],
                                       start=e == 0, stop=e == KD - 1)
                    mm.then_inc(setup_wov, 1)
                pe.wait_ge(setup_dve, 9)

            def project(kind, weights_h, weights_l):
                def do(pair, e):
                    key = (kind, e)
                    b = pb[e % 2]
                    take(b, pair, key)
                    c = slice(e * P, (e + 1) * P)
                    if kind == "V":
                        ops = [(xt_h[:, k, c], xt_l[:, k, c], weights_h[:, k, :], weights_l[:, k, :]) for k in range(KD)]
                    else:
                        ops = [(weights_h[:, k, c], weights_l[:, k, c], xt_h[:, k, :], xt_l[:, k, :]) for k in range(KD)]
                    if key == ("ZL", 0):
                        if first(pair):
                            pe.wait_ge(setup_dve, 1)
                        pe.wait_ge(xt_lo.sem, xt_lo.after(pair, ("XT", 0)))
                    split_product(b.t[:], ops[:2], True, False)
                    if key == ("ZL", 0):
                        pe.wait_ge(xt_lo.sem, xt_lo.after(pair, ("XT", 1)))
                    split_product(b.t[:], ops[2:], False, True).then_inc(b.full, 1)
                return do

            def gram(kind, z):
                def do(pair, h):
                    key = (kind, h)
                    b = gb[h]
                    take(b, pair, key)
                    for n in (2, 3):
                        pe.wait_ge(pb[n % 2].free, pb[n % 2].read(pair, (z, n)))
                    m = slice(h * N, (h + 1) * N)
                    for j in range(NT):
                        c = slice(h * N + j * P, h * N + (j + 1) * P)
                        mm = split_product(b.t[:, j * N:(j + 1) * N],
                                           [(z_h[:, k, c], z_l[:, k, c], z_h[:, k, m], z_l[:, k, m]) for k in range(KD)],
                                           True, True)
                    mm.then_inc(b.full, 1)
                return do

            def spread(outap, col):
                return pe.transpose(outap, col.broadcast_to([P, P]), ident[:])

            def rb(pair, h):
                take(pb[h], pair, ("RB", h))
                pe.wait_ge(lang_r.sem, lang_r.after(pair, ("GL", h)))
                for j in range(NT):
                    mm = spread(pb[h].t[:, j * P:(j + 1) * P], cols[:, h, R, j:j + 1])
                mm.then_inc(pb[h].full, 1)

            def hb(pair, h):
                take(pb[h], pair, ("HB", h))
                pe.wait_ge(grav_hsq.sem, grav_hsq.after(pair, ("GG", h)))
                for j in range(NT):
                    mm = spread(pb[h].t[:, j * P:(j + 1) * P], cols[:, h, HSQ, j:j + 1])
                mm.then_inc(pb[h].full, 1)

            def kt(pair, h):
                take(pb[h], pair, ("KT", h))
                pe.wait_ge(graph.sem, graph.after(pair, ("EG", h)))
                for mt in range(NT):
                    for j in range(NT):
                        mm = pe.transpose(pb[h].t[:, mt * N + j * P:mt * N + (j + 1) * P],
                                          lang[:, h, j, mt * P:(mt + 1) * P], ident[:])
                mm.then_inc(pb[h].full, 1)

            def kv(pair, h):
                pe.wait_ge(pb[h].free, pb[h].read(pair, ("KT", h)))
                for j in range(NT):
                    b = (gb, pb)[h][j]
                    take(b, pair, ("KV", h))
                    c = slice(j * P, (j + 1) * P)
                    split_product(b.t[:], [(kt_h[:, h, mt, c], kt_l[:, h, mt, c], v_h[:, NT * h + mt, :],
                                            v_l[:, NT * h + mt, :]) for mt in range(NT)],
                                  True, True).then_inc(b.full, 1)

            def y(pair, layer, h, which):
                for j in range(NT):
                    if layer == 0:
                        pe.wait_ge(x_lo[0][j].sem, x_lo[0][j].after(pair, (("KVN", "KVL")[j], h)))
                    else:
                        pe.wait_ge(x_lo[1][j].sem, x_lo[1][j].after(pair, (("NRM", "LOW")[j], 0, h)))
                m = slice(0, YW) if layer == 0 else slice(2, 2 + YW)
                for i in (0, 1) if which == "YA" else (2, 3):
                    b = yb[i % 2]
                    take(b, pair, (which, layer, h))
                    c = slice(i * P, (i + 1) * P)
                    split_product(b.t[:, 0:YW], [(x_h[:, NT * h + t, c], x_l[:, NT * h + t, c], aq_h[:, t, m], aq_l[:, t, m])
                                                 for t in range(NT)], True, True).then_inc(b.full, 1)

            def qk_rows(pair, layer, h):
                key = ("QK", layer, h)
                pe.wait_ge(qk_cols.sem, qk_cols.after(pair, ("YB", layer, h)))
                for w in range(2):
                    take(yb[w], pair, key)
                    for i in range(KD):
                        mm = spread(yb[w].t[:, i * P:(i + 1) * P], qk[:, h, i, w:w + 1])
                    mm.then_inc(yb[w].full, 1)

            def apply(pair, layer, h, c):
                for i in (2 * c, 2 * c + 1):
                    pe.wait_ge(att_lo.sem, att_lo.after(pair, ("AL", layer, h, c), i % 2 + 1))
                    for ot in range(NT):
                        if i == 0:
                            take(ub[ot], pair, ("U", layer, h, 1))
                        m = y_cols(layer, ot)
                        mm = split_product(ub[ot].t[:], [(y_h[:, h, i, m], y_l[:, h, i, m], att_h[:, i, :], att_l[:, i, :])],
                                           i == 0, i == KD - 1)
                        if i == KD - 1:
                            mm.then_inc(ub[ot].full, 1)

            def den(pair, layer, h):
                take(yb[0], pair, ("DEN", layer, h))
                pe.wait_ge(den_lo.sem, den_lo.after(pair, ("DL", layer, h)))
                pe.matmul(yb[0].t[:], ones[:], den_h[:], start=True, stop=False)
                pe.matmul(yb[0].t[:], ones[:], den_l[:], start=False, stop=True).then_inc(yb[0].full, 1)

            def l3(pair, h):
                for j in range(NT):
                    pe.wait_ge(x_lo[1][j].sem, x_lo[1][j].after(pair, (("NRM", "LOW")[j], 1, h)))
                for mt in range(NT):
                    take(ub[mt], pair, ("L3", h))
                    c = slice(mt * P, (mt + 1) * P)
                    split_product(ub[mt].t[:], [(a2_h[:, t, c], a2_l[:, t, c], x_h[:, NT * h + t, :], x_l[:, NT * h + t, :])
                                                for t in range(NT)], True, True).then_inc(ub[mt].full, 1)

            schedule(pe, "PE", {"ZL": project("ZL", wl_h, wl_l), "ZG": project("ZG", wg_h, wg_l), "V": project("V", wv_h, wv_l),
                          "GL": gram("GL", "ZL"), "GG": gram("GG", "ZG"), "RB": rb, "HB": hb, "KT": kt, "KV": kv,
                          "YA": half_of(y, "YA"), "YB": half_of(y, "YB"), "QK": qk_rows, "U": apply, "DEN": den, "L3": l3}, ((), ()), setup)

        @block.scalar
        def _(act):
            nc.scalar.preload_act_table_set("natural_log_exp_and_others")
            def split_w_lang():
                act.wait_ge(wl_in, 16)
                nc.scalar.activation(wl_h[:], att[:], ACT.Copy).then_inc(setup_act, 1)

            def setup():
                act.wait_ge(small_in, 16 * 8)
                nc.scalar.activation(aq_h[:], small_view(u, NT, AQ), ACT.Copy).then_inc(setup_act, 1)
                nc.scalar.activation(tiny[:, 2:3], tiny[:, 0:1], ACT.Exp, scale=-1.0).then_inc(setup_act, 1)
                nc.scalar.activation(inv_s2[:], tiny[:, 1:2], ACT.Exp, scale=-2.0).then_inc(setup_act, 1)
                act.wait_ge(wg_in, 16)
                nc.scalar.activation(wg_h[:], att[:], ACT.Copy).then_inc(setup_act, 1)
                act.wait_ge(setup_dve, 4)
                nc.scalar.activation(a2_h[:], grav[:, 0, :, :], ACT.Copy).then_inc(setup_act, 1)
                for k in range(KD):
                    act.wait_ge(setup_wov, k + 1)
                    nc.scalar.activation(wv_h[:, k, :], (gb + ub)[k].t[:], ACT.Copy).then_inc(setup_act, 1)

            def xt_split(pair, c):
                act.wait_ge(xt_loaded.sem, xt_loaded.after(pair, ("XT", c)))
                if not first(pair):
                    last = max((("ZG", 3), ("V", 3)), key=ORDERS["PE"].index)
                    act.wait_ge(pb[1].full, pb[1].filled(pair - 1, last))
                nc.scalar.activation(xt_h[:, 2 * c:2 * c + 2, :], xt_in[:], ACT.Copy).then_inc(xt_hi.sem, 1)
                if first(pair) and c == 0:
                    split_w_lang()

            def project(kind, dst):
                def do(pair, e):
                    b = pb[e % 2]
                    act.wait_ge(b.full, b.filled(pair, (kind, e)))
                    if kind == "ZG":
                        act.wait_ge(gb[1].full, gb[1].filled(pair, ("GL", 1)))
                    elif kind == "ZL" and not first(pair):
                        act.wait_ge(gb[1].full, gb[1].filled(pair - 1, ("GG", 1)))
                    elif kind == "V" and not first(pair):
                        act.wait_ge(pb[1].full, pb[1].filled(pair - 1, ("KV", 1)))
                    nc.scalar.activation(dst[:, e, :], b.t[:], ACT.Copy).then_inc(proj_hi.sem, 1)
                return do

            def gl(pair, h):
                act.wait_ge(lang_sq.sem, lang_sq.after(pair, ("GL", h)))
                act_f.link(act, nc.scalar.activation(cols[:, h, LNS, :], cols[:, h, SS, :], ACT.Ln))
                nc.scalar.activation(cols[:, h, R, :], cols[:, h, LNS, :], ACT.Exp, scale=-0.5).then_inc(lang_r.sem, 1)

            def hb(pair, h):
                act.wait_ge(pb[h].full, pb[h].filled(pair, ("HB", h)))
                nc.scalar.activation(half_sq_bc[:, h, :], pb[h].t[:, 0:N], ACT.Copy).then_inc(pb[h].free, 1)
                act.wait_ge(gb[h].free, gb[h].read(pair, ("GG", h)))
                act_f.link(act, nc.scalar.activation(grav[:, h, :, :], grav[:, h, :, :], ACT.Relu, scale=-1.0))
                nc.scalar.activation(grav[:, h, :, :], grav[:, h, :, :], ACT.Exp, scale=neg_inv_s2[:, 0:1]).then_inc(grav_e.sem, 1)

            def kt(pair, h):
                act.wait_ge(pb[h].full, pb[h].filled(pair, ("KT", h)))
                nc.scalar.activation(kt_h[:, h, :, :], pb[h].t[:].rearrange("p (t n) -> p t n", t=NT),
                                     ACT.Copy).then_inc(kt_hi.sem, 1)

            def rstd_of(s, chain, pair, key, h):
                act.wait_ge(var_known[s].sem, var_known[s].after(pair, key))
                chain.link(act, nc.scalar.activation(log_var[:, s, h, :], mean_var[:, s, h, :, 1], ACT.Ln, bias=eps_col[:, 0:1]))
                nc.scalar.activation(rstd[:, s, h, :], log_var[:, s, h, :], ACT.Exp, scale=-0.5).then_inc(rstd_known[s].sem, 1)

            def kv(pair, h):
                rstd_of(0, act_f, pair, ("KV", h), h)

            def x_split(s, pair, key, h, src):
                for j in range(NT):
                    act.wait_ge(normed[s].sem, normed[s].after(pair, key, j + 1))
                    nc.scalar.activation(x_h[:, NT * h + j, :], src[:, NT * h + j, :], ACT.Copy).then_inc(x_hi[s].sem, 1)

            def kvn(pair, h):
                if not first(pair):
                    act.wait_ge(ub[1].full, ub[1].filled(pair - 1, ("L3", h)))
                x_split(0, pair, ("KVN", h), h, x1)

            def y(pair, layer, h, which):
                for i in (0, 1) if which == "YA" else (2, 3):
                    b = yb[i % 2]
                    act.wait_ge(b.full, b.filled(pair, (which, layer, h)))
                    if i == 0 and layer == 1:
                        act.wait_ge(ub[1].full, ub[1].filled(pair, ("U", 0, h, 1)))
                    elif i == 0 and not first(pair):
                        act.wait_ge(ub[1].full, ub[1].filled(pair - 1, ("U", 1, h, 1)))
                    nc.scalar.activation(y_h[:, h, i, :], b.t[:, 0:YW], ACT.Copy).then_inc(y_hi.sem, 1)

            def qk_rows(pair, layer, h):
                act.wait_ge(q_max.sem, q_max.after(pair, ("QK", layer, h)))
                last = before(pair, layer, h)
                if last:
                    act.wait_ge(att_val.sem, att_val.after(last[0], ("AV",) + last[1:] + (1,)))
                act.wait_ge(yb[1].full, yb[1].filled(pair, ("QK", layer, h)))
                act_b.link(act, nc.scalar.activation(s_pos[:], yb[1].t[:], ACT.Relu, bias=qs[:, h, 0:1]))
                nc.scalar.activation(s_neg[:], yb[1].t[:], ACT.Relu, bias=qs[:, h, 1:2], scale=-1.0).then_inc(yb[1].free, 1)
                act.wait_ge(yb[1].free, yb[1].read(pair, ("QK", layer, h)))
                nc.scalar.activation(s_pos[:], s_pos[:], ACT.Exp, scale=-(1.0 - LEAK))
                nc.scalar.activation(s_neg[:], s_neg[:], ACT.Exp, scale=-(1.0 - LEAK))
                nc.scalar.activation(ab[:, h, 0, :], qs[:, h, 2:2 + KD], ACT.Exp)
                nc.scalar.activation(ab[:, h, 1, :], qs[:, h, 2:2 + KD], ACT.Exp, scale=LEAK).then_inc(factors.sem, 1)

            def att_b(pair, layer, h):
                last = before(pair, layer, h)
                if last:
                    act.wait_ge(att_lo.sem, att_lo.after(last[0], ("AL",) + last[1:] + (1,)))
                    act.wait_ge(summed.sem, summed.after(last[0], ("DS",) + last[1:]))
                else:
                    act.wait_ge(setup_dve, 8)
                act.wait_ge(factors.sem, factors.after(pair, ("QK", layer, h)))
                for i in range(KD):
                    nc.scalar.activation(att[:, i, :], s_pos[:], ACT.Copy, scale=ab[:, h, 1, i:i + 1]).then_inc(att_low.sem, 1)

            def att_split(pair, layer, h, c):
                last = before(pair, layer, h)
                if last and c == 0:
                    act.wait_ge(ub[1].full, ub[1].filled(last[0], ("U",) + last[1:] + (1,)))
                for i in (2 * c, 2 * c + 1):
                    act.wait_ge(att_val.sem, att_val.after(pair, ("AV", layer, h, c), i % 2 + 1))
                    nc.scalar.activation(att_h[:, i, :], att[:, i, :], ACT.Copy).then_inc(att_hi.sem, 1)

            def den_split(pair, layer, h):
                act.wait_ge(summed.sem, summed.after(pair, ("DS", layer, h)))
                nc.scalar.activation(den_h[:], den_sum[:], ACT.Copy).then_inc(den_hi.sem, 1)

            def den(pair, layer, h):
                act.wait_ge(yb[0].full, yb[0].filled(pair, ("DEN", layer, h)))
                last = before(pair, layer, h)
                if last:
                    act.wait_ge(ub[1].free, ub[1].read(last[0], ("U",) + last[1:] + (1,)))
                nc.scalar.activation(inv_den_bc[:], yb[0].t[:], ACT.Ln).then_inc(yb[0].free, 1)
                act.wait_ge(yb[0].free, yb[0].read(pair, ("DEN", layer, h)))
                nc.scalar.activation(inv_den_bc[:], inv_den_bc[:], ACT.Exp, scale=-1.0).then_inc(inverted.sem, 1)

            def res(pair, layer, h):
                for ot in range(NT):
                    act.wait_ge(ub[ot].free, ub[ot].read(pair, ("U", layer, h, 1)))
                    nc.scalar.activation(u[:, ot, :], u[:, ot, :], ACT.Relu, bias=bm[:, layer, ot:ot + 1]).then_inc(relued.sem, 1)

            def sta(pair, layer, h):
                rstd_of(1, act_b, pair, ("STA", layer, h), h)

            def nrm(pair, layer, h):
                x_split(1, pair, ("NRM", layer, h), h, x2)

            def l3(pair, h):
                rstd_of(1, act_b, pair, ("L3", h), h)

            schedule(act, "ACT", {"XT": xt_split, "ZL": project("ZL", z_h), "ZG": project("ZG", z_h), "V": project("V", v_h),
                           "GL": gl, "HB": hb, "KT": kt, "KV": kv, "KVN": kvn, "YA": half_of(y, "YA"), "YB": half_of(y, "YB"), "QK": qk_rows,
                           "AT": att_b, "AH": att_split, "DH": den_split, "DEN": den, "RES": res, "STA": sta, "NRM": nrm, "L3": l3}, ((act_f,), (act_b,)), setup)

        @block.vector
        def _(dve):
            sub, mult, add, vmax = ALU.subtract, ALU.mult, ALU.add, ALU.max
            nc.vector.memset(eps_col[:], LN_EPS)
            dve.wait_ge(wl_in, 16)
            dve.wait_ge(setup_act, 1)
            nc.vector.tensor_tensor(wl_l[:], att[:], f32(wl_h[:]), sub).then_inc(setup_dve, 1)

            def setup():
                dve.wait_ge(small_in, 16 * 8)
                nc.vector.tensor_scalar(ones[:], ident[:], 0.0, 1.0, mult, add).then_inc(setup_dve, 1)
                dve.wait_ge(setup_act, 4)
                nc.vector.tensor_scalar(tiny[:, 3:4], tiny[:, 2:3], 1.0, None, add).then_inc(setup_dve, 1)
                nc.vector.tensor_tensor(grav[:, 0, :, :], offdiag[:], offdiag[:], mult).then_inc(setup_dve, 1)
                nc.vector.tensor_tensor(aq_l[:], small_view(u, NT, AQ), f32(aq_h[:]), sub).then_inc(setup_dve, 1)
                dve.wait_ge(setup_dve, 4)
                nc.vector.reciprocal(w_lang_col[:], tiny[:, 3:4]).then_inc(setup_dve, 1)
                for j in range(NT):
                    d = offdiag[:, j, j * P:(j + 1) * P]
                    own = lang[:, 0, j, 0:P]
                    nc.vector.tensor_scalar(own, ident[:], -1.0, 1.0, mult, add).then_inc(setup_own, 1)
                    dve.wait_ge(setup_own, 2 * j + 1)
                    nc.vector.tensor_tensor(d, d, own, mult).then_inc(setup_own, 1)
                dve.wait_ge(setup_dve, 6)
                nc.vector.tensor_scalar(neg_inv_s2[:], inv_s2[:], -1.0, None, mult)
                nc.vector.tensor_scalar(w_grav_col[:], w_lang_col[:], -1.0, 1.0, mult, add).then_inc(setup_own, 1)
                dve.wait_ge(setup_own, 5)
                dve.wait_ge(wg_in, 16)
                dve.wait_ge(setup_act, 5)
                nc.vector.tensor_tensor(wg_l[:], att[:], f32(wg_h[:]), sub).then_inc(setup_dve, 1)
                dve.wait_ge(setup_act, 6)
                nc.vector.tensor_tensor(a2_l[:], grav[:, 0, :, :], f32(a2_h[:]), sub).then_inc(setup_dve, 1)
                for k in range(KD):
                    dve.wait_ge(setup_act, 7 + k)
                    mm = nc.vector.tensor_tensor(wv_l[:, k, :], (gb + ub)[k].t[:], f32(wv_h[:, k, :]), sub)
                mm.then_inc(setup_dve, 1)
                dve.wait_ge(setup_dve, 9)

            def project(kind, dst_h, dst_l):
                def do(pair, e):
                    b = pb[e % 2]
                    dve.wait_ge(proj_hi.sem, proj_hi.after(pair, (kind, e)))
                    nc.vector.tensor_tensor(dst_l[:, e, :], b.t[:], f32(dst_h[:, e, :]), sub).then_inc(b.free, 1)
                return do

            def diagonal(b, h, to, scratch):
                for j in range(NT):
                    ins = nc.vector.scalar_tensor_tensor(scratch[:, h, j, 0:P], b.t[:, j * N + j * P:j * N + (j + 1) * P], 1.0,
                                                         ident[:], mult, mult, accum_out=cols[:, h, to, j:j + 1])
                dve_f.link(dve, ins)

            def gl(pair, h):
                b = gb[h]
                dve.wait_ge(b.full, b.filled(pair, ("GL", h)))
                if not first(pair):
                    dve.wait_ge(pb[h].full, pb[h].filled(pair - 1, ("KT", h)))
                diagonal(b, h, SS, lang)
                nc.vector.tensor_scalar(cols[:, h, SS, :], cols[:, h, SS, :], EPS * EPS, None, vmax).then_inc(lang_sq.sem, 1)
                nc.vector.scalar_tensor_tensor(lang[:, h, :, :], b.t[:].rearrange("p (t n) -> p t n", t=NT), 0.0, offdiag[:],
                                               vmax, mult).then_inc(b.free, 1)
                dve.wait_ge(b.free, b.read(pair, ("GL", h)))

            def row_factor(h, deg, to, weight):
                dve_f.link(dve, nc.vector.tensor_scalar(cols[:, h, deg, :], cols[:, h, deg, :], EPS, None, vmax))
                dve_f.link(dve, nc.vector.reciprocal(cols[:, h, to, :], cols[:, h, deg, :]))
                dve_f.link(dve, nc.vector.tensor_scalar(cols[:, h, to, :], cols[:, h, to, :], weight[:, 0:1], None, mult))

            def rb(pair, h):
                b = pb[h]
                dve.wait_ge(b.full, b.filled(pair, ("RB", h)))
                for j in range(NT):
                    ins = nc.vector.scalar_tensor_tensor(lang[:, h, j, :], lang[:, h, j, :], cols[:, h, R, j:j + 1], b.t[:, 0:N],
                                                         mult, mult, accum_out=cols[:, h, DEGL, j:j + 1])
                ins.then_inc(b.free, 1)
                dve.wait_ge(b.free, b.read(pair, ("RB", h)))
                row_factor(h, DEGL, CL, w_lang_col)

            def gg(pair, h):
                b = gb[h]
                dve.wait_ge(b.full, b.filled(pair, ("GG", h)))
                diagonal(b, h, SQ, grav)
                nc.vector.tensor_scalar(cols[:, h, HSQ, :], cols[:, h, SQ, :], 0.5, None, mult).then_inc(grav_hsq.sem, 1)

            def hb(pair, h):
                b = gb[h]
                dve.wait_ge(pb[h].free, pb[h].read(pair, ("HB", h)))
                dve.wait_ge(grav_hsq.sem, grav_hsq.after(pair, ("GG", h)))
                for j in range(NT):
                    ins = nc.vector.scalar_tensor_tensor(grav[:, h, j, :], b.t[:, j * N:(j + 1) * N], cols[:, h, HSQ, j:j + 1],
                                                         half_sq_bc[:, h, :], sub, sub)
                ins.then_inc(b.free, 1)

            def eg(pair, h):
                dve.wait_ge(grav_e.sem, grav_e.after(pair, ("HB", h)))
                for j in range(NT):
                    ins = nc.vector.scalar_tensor_tensor(grav[:, h, j, :], grav[:, h, j, :], 1.0, offdiag[:, j, :], mult, mult,
                                                         accum_out=cols[:, h, DEGG, j:j + 1])
                dve_f.link(dve, ins)
                row_factor(h, DEGG, CG, w_grav_col)
                for j in range(NT):
                    ins = nc.vector.tensor_scalar(grav[:, h, j, :], grav[:, h, j, :], cols[:, h, CG, j:j + 1], None, mult)
                dve_f.link(dve, ins)
                for j in range(NT):
                    ins = nc.vector.scalar_tensor_tensor(lang[:, h, j, :], lang[:, h, j, :], cols[:, h, CL, j:j + 1],
                                                         grav[:, h, j, :], mult, add)
                ins.then_inc(graph.sem, 1)

            def kt(pair, h):
                dve.wait_ge(kt_hi.sem, kt_hi.after(pair, ("KT", h)))
                nc.vector.tensor_tensor(kt_l[:, h, :, :], pb[h].t[:].rearrange("p (t n) -> p t n", t=NT), f32(kt_h[:, h, :, :]),
                                        sub).then_inc(pb[h].free, 1)

            def low(s, pair, key, h, src):
                dve.wait_ge(x_hi[s].sem, x_hi[s].after(pair, key, 2))
                t = NT * h + 1
                nc.vector.tensor_tensor(x_l[:, t, :], src[:, t, :], f32(x_h[:, t, :]), sub).then_inc(x_lo[s][1].sem, 1)

            def normalise(s, pair, stat_key, key, h, x):
                dve.wait_ge(rstd_known[s].sem, rstd_known[s].after(pair, stat_key))
                for j in range(NT):
                    t = x[:, NT * h + j, :]
                    nc.vector.tensor_scalar(t, t, mean_var[:, s, h, j, 0:1], rstd[:, s, h, j:j + 1], sub,
                                            mult).then_inc(normed[s].sem, 1)

            def kv(pair, h):
                dve.wait_ge(x0_loaded[h], 16 * pair + 16)
                for j in range(NT):
                    b = (gb, pb)[h][j]
                    t = x1[:, NT * h + j, :]
                    dve.wait_ge(b.full, b.filled(pair, ("KV", h)))
                    nc.vector.tensor_tensor(t, b.t[:], t, add).then_inc(b.free, 1)
                    dve.wait_ge(b.free, b.read(pair, ("KV", h)))
                for j in range(NT):
                    ins = nc.vector.bn_stats(stats[:, 0, h, j, :], x1[:, NT * h + j, :])
                dve_f.link(dve, ins)
                dve_carrier()
                for j in range(NT):
                    ins = nc.vector.bn_aggr(mean_var[:, 0, h, j, :], stats[:, 0, h, j, :])
                ins.then_inc(var_known[0].sem, 1)

            def kvn(pair, h):
                normalise(0, pair, ("KV", h), ("KVN", h), h, x1)

            def kvl(pair, h):
                low(0, pair, ("KVN", h), h, x1)

            def y(pair, layer, h, which):
                for i in (0, 1) if which == "YA" else (2, 3):
                    b = yb[i % 2]
                    dve.wait_ge(y_hi.sem, y_hi.after(pair, (which, layer, h), i % 2 + 1))
                    nc.vector.tensor_tensor(y_l[:, h, i, :], b.t[:, 0:YW], f32(y_h[:, h, i, :]), sub).then_inc(b.free, 1)
                if which == "YA":
                    return
                for n in range(2):
                    dve.wait_ge(yb[n].free, yb[n].read(pair, ("YB", layer, h)))
                c = q_cols(layer)
                nc.vector.tensor_tensor(qk[:, h, :, :], f32(y_h[:, h, :, c]), f32(y_l[:, h, :, c]), add).then_inc(qk_cols.sem, 1)

            def qk_rows(pair, layer, h):
                b = yb[0]
                dve.wait_ge(b.full, b.filled(pair, ("QK", layer, h)))
                nc.vector.reduce_max(qs[:, h, 0:1], b.t[:], AX_X).then_inc(b.free, 1)
                dve.wait_ge(b.free, b.read(pair, ("QK", layer, h)))
                nc.vector.tensor_scalar(qs[:, h, 1:2], qs[:, h, 0:1], -1.0, None, mult)
                nc.vector.tensor_scalar(qs[:, h, 2:2 + KD], qk[:, h, :, 0], qs[:, h, 0:1], None, sub).then_inc(q_max.sem, 1)

            def att_value(pair, layer, h, c):
                for i in (2 * c, 2 * c + 1):
                    dve.wait_ge(att_low.sem, att_low.after(pair, ("AT", layer, h), i + 1))
                    nc.vector.scalar_tensor_tensor(att[:, i, :], s_neg[:], ab[:, h, 0, i:i + 1], att[:, i, :], mult,
                                                   vmax).then_inc(att_val.sem, 1)

            def att_low_part(pair, layer, h, c):
                for i in (2 * c, 2 * c + 1):
                    dve.wait_ge(att_hi.sem, att_hi.after(pair, ("AH", layer, h, c), i % 2 + 1))
                    nc.vector.tensor_tensor(att_l[:, i, :], att[:, i, :], f32(att_h[:, i, :]), sub).then_inc(att_lo.sem, 1)

            def res(pair, layer, h):
                dve.wait_ge(inverted.sem, inverted.after(pair, ("DEN", layer, h)))
                for ot in range(NT):
                    b = ub[ot]
                    dve.wait_ge(b.full, b.filled(pair, ("U", layer, h, 1)))
                    nc.vector.tensor_tensor(u[:, ot, :], b.t[:], inv_den_bc[:], mult).then_inc(b.free, 1)

            def sta(pair, layer, h):
                if layer == 0 and not first(pair):
                    dve.wait_ge(stored[h], 16 * pair)
                src = x1 if layer == 0 else x2
                dve.wait_ge(relued.sem, relued.after(pair, ("RES", layer, h), 2))
                nc.vector.tensor_tensor(x2[:, NT * h + 1, :], u[:, 1, :], src[:, NT * h + 1, :], add).then_inc(added[1].sem, 1)
                for j in (1, 0):
                    dve.wait_ge(added[j].sem, added[j].after(pair, (("RES", "STA")[j], layer, h)))
                    ins = nc.vector.bn_stats(stats[:, 1, h, j, :], x2[:, NT * h + j, :])
                dve_b.link(dve, ins)
                dve_carrier()
                for j in range(NT):
                    ins = nc.vector.bn_aggr(mean_var[:, 1, h, j, :], stats[:, 1, h, j, :])
                ins.then_inc(var_known[1].sem, 1)

            def nrm(pair, layer, h):
                normalise(1, pair, ("STA", layer, h), ("NRM", layer, h), h, x2)

            def nrm_low(pair, layer, h):
                low(1, pair, ("NRM", layer, h), h, x2)

            def l3(pair, h):
                for mt in range(NT):
                    b = ub[mt]
                    t = x2[:, NT * h + mt, :]
                    dve.wait_ge(b.full, b.filled(pair, ("L3", h)))
                    dve.wait_ge(biased.sem, biased.after(pair, ("NRM", 1, h), mt + 1))
                    nc.vector.tensor_tensor(t, b.t[:], t, add).then_inc(b.free, 1)
                    dve.wait_ge(b.free, b.read(pair, ("L3", h)))
                    ins = nc.vector.bn_stats(stats[:, 1, h, mt, :], t)
                dve_b.link(dve, ins)
                dve_carrier()
                for j in range(NT):
                    ins = nc.vector.bn_aggr(mean_var[:, 1, h, j, :], stats[:, 1, h, j, :])
                ins.then_inc(var_known[1].sem, 1)

            def l3n(pair, h):
                normalise(1, pair, ("L3", h), ("L3N", h), h, x2)

            schedule(dve, "DVE", {"ZL": project("ZL", z_h, z_l), "ZG": project("ZG", z_h, z_l),
                           "V": project("V", v_h, v_l), "GL": gl, "RB": rb, "GG": gg, "HB": hb, "EG": eg, "KT": kt,
                           "KV": kv, "KVN": kvn, "KVL": kvl, "YA": half_of(y, "YA"), "YB": half_of(y, "YB"), "QK": qk_rows, "AV": att_value, "AL": att_low_part, "RES": res,
                           "STA": sta, "NRM": nrm, "LOW": nrm_low, "L3": l3, "L3N": l3n}, ((dve_f,), (dve_b,)), setup)

        @block.gpsimd
        def _(pool):
            def sums(pair, layer, h):
                last = before(pair, layer, h)
                if last:
                    pool.wait_ge(yb[0].full, yb[0].filled(last[0], ("DEN",) + last[1:]))
                pool.wait_ge(att_val.sem, att_val.after(pair, ("AV", layer, h, 0), 2))
                pool_b.link(pool, nc.gpsimd.tensor_tensor(den_sum[:], att[:, 0, :], att[:, 1, :], ALU.add))
                pool.wait_ge(att_val.sem, att_val.after(pair, ("AV", layer, h, 1), 1))
                pool_b.link(pool, nc.gpsimd.tensor_tensor(den_sum[:], den_sum[:], att[:, 2, :], ALU.add))
                pool.wait_ge(att_val.sem, att_val.after(pair, ("AV", layer, h, 1), 2))
                nc.gpsimd.tensor_tensor(den_sum[:], den_sum[:], att[:, 3, :], ALU.add).then_inc(summed.sem, 1)

            def sums_low(pair, layer, h):
                pool.wait_ge(den_hi.sem, den_hi.after(pair, ("DH", layer, h)))
                nc.gpsimd.tensor_tensor(den_l[:], den_sum[:], f32(den_h[:]), ALU.subtract).then_inc(den_lo.sem, 1)

            def xt_split(pair, c):
                pool.wait_ge(xt_hi.sem, xt_hi.after(pair, ("XT", c)))
                k = slice(2 * c, 2 * c + 2)
                nc.gpsimd.tensor_tensor(xt_l[:, k, :], xt_in[:], f32(xt_h[:, k, :]), ALU.subtract).then_inc(xt_lo.sem, 1)

            def low(s, pair, key, h, src):
                pool.wait_ge(x_hi[s].sem, x_hi[s].after(pair, key, 1))
                t = NT * h
                nc.gpsimd.tensor_tensor(x_l[:, t, :], src[:, t, :], f32(x_h[:, t, :]), ALU.subtract).then_inc(x_lo[s][0].sem, 1)

            def res(pair, layer, h):
                if layer == 0 and not first(pair):
                    pool.wait_ge(stored[h], 16 * pair)
                src = x1 if layer == 0 else x2
                pool.wait_ge(relued.sem, relued.after(pair, ("RES", layer, h), 1))
                nc.gpsimd.tensor_tensor(x2[:, NT * h, :], u[:, 0, :], src[:, NT * h, :], ALU.add).then_inc(added[0].sem, 1)

            def kvn(pair, h):
                low(0, pair, ("KVN", h), h, x1)

            def nrm(pair, layer, h):
                low(1, pair, ("NRM", layer, h), h, x2)
                if layer == 1:
                    for j in range(NT):
                        pool.wait_ge(x_lo[1][j].sem, x_lo[1][j].after(pair, (("NRM", "LOW")[j], 1, h)))
                        t = x2[:, NT * h + j, :]
                        nc.gpsimd.tensor_tensor(t, t, bias_bc[:], ALU.add).then_inc(biased.sem, 1)

            schedule(pool, "POOL", {"XT": xt_split, "DS": sums, "DL": sums_low, "RES": res, "KVN": kvn, "NRM": nrm}, ((), (pool_b,)))


def small_view(t, a, b):
    return t[:].rearrange("p c n -> p (c n)")[:, 0:a * b].rearrange("p (a b) -> p a b", a=a)


def kernel(x, adj, L0_gnn_W_lang, L0_gnn_W_grav, L0_gnn_W_V, L0_gnn_W_O, L0_gnn_gate_logit, L0_gnn_log_sigma,
           L1_gnn_wq, L1_gnn_wk, L1_gnn_bm, L2_gnn_wq, L2_gnn_wk, L2_gnn_bm, L3_gnn_bias):
    import numpy as np
    import concourse.bacc as bacc
    from concourse.bass_utils import run_bass_kernel_spmd

    a = {k: np.asarray(v) for k, v in locals().items() if k not in ("np", "bacc", "run_bass_kernel_spmd")}
    B, N, D = a["x"].shape
    PAIRS, NT, KD = B // 2, N // P, D // P
    col = lambda v: np.ascontiguousarray(v.reshape(-1, P).T)
    adj_t = a["adj"].T
    arrays = {
        "xn": np.ascontiguousarray(a["x"].reshape(PAIRS, 2 * NT, P, D).transpose(0, 2, 1, 3)),
        "xt": np.ascontiguousarray(a["x"].reshape(PAIRS, 2 * N, KD, P).transpose(0, 3, 2, 1)),
        "adj": np.ascontiguousarray(a["adj"]),
        "adjq": np.ascontiguousarray(np.concatenate(
            [a["L1_gnn_wq"][:, None], a["L1_gnn_wk"][:, None], adj_t, a["L2_gnn_wq"][:, None], a["L2_gnn_wk"][:, None]], axis=1)),
        "w_l": np.ascontiguousarray(a["L0_gnn_W_lang"].T),
        "w_g": np.ascontiguousarray(a["L0_gnn_W_grav"].T),
        "w_v": np.ascontiguousarray(a["L0_gnn_W_V"]),
        "w_o": np.ascontiguousarray(a["L0_gnn_W_O"].T),
        "gate": np.ascontiguousarray(np.broadcast_to(a["L0_gnn_gate_logit"].reshape(1, 1), (P, 1))),
        "sigma": np.ascontiguousarray(np.broadcast_to(a["L0_gnn_log_sigma"].reshape(1, 1), (P, 1))),
        "bm1": col(a["L1_gnn_bm"]),
        "bm2": col(a["L2_gnn_bm"]),
        "bias3": np.ascontiguousarray(np.broadcast_to(a["L3_gnn_bias"][None, :], (P, D))),
        "ident": np.eye(P, dtype=np.float32),
    }
    nc = bacc.Bacc("TRN2", target_bir_lowering=False, num_devices=1, dynamic_dma_scratch_size=1024)
    args = [nc.dram_tensor(f"in_{k}", v.shape, mybir.dt.from_np(v.dtype), kind="ExternalInput").ap() for k, v in arrays.items()]
    args.append(nc.dram_tensor("out", (PAIRS, P, 2 * NT, D), F32, kind="ExternalOutput").ap())
    resnorm_kernel(nc, *args)
    r = run_bass_kernel_spmd(nc, [{f"in_{k}": v for k, v in arrays.items()}], core_ids=[0])
    got = r.results[0]["out"]
    return np.ascontiguousarray(got.transpose(0, 2, 1, 3)).reshape(B, N, D)
```
